# Optimizing a Trainium2 kernel written in Bass

```python
import numpy as np
import jax
import jax.numpy as jnp

def _softmax(x, axis=-1):
    return jax.nn.softmax(x, axis=axis)

def _gelu(x):
    return jax.nn.gelu(x, approximate=True)

def _silu(x):
    return jax.nn.silu(x)

def _sigmoid(x):
    return jax.nn.sigmoid(x)

def _layernorm(x, axis=-1, eps=1e-05):
    m = jnp.mean(x, axis=axis, keepdims=True)
    v = jnp.var(x, axis=axis, keepdims=True)
    return (x - m) / jnp.sqrt(v + eps)

def _scatter_add(tgt, idx, src, axis=0):
    return tgt.at[idx].add(src)

def _segment_sum(src, seg, n):
    return jax.ops.segment_sum(src, seg, n)
kernel_name = 'mk_perceiver_d1_seqx_r4_99ac55'

def setup_inputs(seed: int=0):
    np.random.seed(seed)
    _w = jnp.asarray

    def _rec_inputs():
        import jax
        import jax.numpy as jnp
        _rk = jax.random.key(seed)
        x = -0.0005146 + 1 * jax.random.normal(jax.random.fold_in(_rk, 1), (1, 128, 256), jnp.float32)
        _lenS = 128 - jax.random.randint(jax.random.fold_in(_rk, 7), (1,), 0, max(1, 128 // 4) + 1, jnp.int32)
        _lenS2 = 12544 - jax.random.randint(jax.random.fold_in(_rk, 8), (1,), 0, max(1, 12544 // 4) + 1, jnp.int32)
        _ctx_768P = jax.random.normal(jax.random.fold_in(_rk, 11), (1, 16, 192), jnp.float32)
        _ctx_768c = jax.random.dirichlet(jax.random.fold_in(_rk, 511), 0.3 * jnp.ones((16,), jnp.float32), (1, 12544))
        _ctx_768t = jnp.einsum('bsk,bkd->bsd', _ctx_768c, _ctx_768P)
        _ctx_768t = _ctx_768t * jax.lax.rsqrt(jnp.mean(jnp.square(_ctx_768t)) + 1e-12) * 0.953939
        ctx_768 = -0.00040386 + 0.999972 * (_ctx_768t + 0.3 * jax.random.normal(jax.random.fold_in(_rk, 611), (1, 12544, 192), jnp.float32))
        _validS = jnp.arange(128)[None, :] < _lenS[:, None]
        _validS2 = jnp.arange(12544)[None, :] < _lenS2[:, None]
        _causal = jnp.tril(jnp.ones((128, 128), dtype=bool))
        mask_BxS2_bk0 = jnp.logical_not(jnp.broadcast_to(_validS2[:, :], (1, 12544)))
        return (x, ctx_768, mask_BxS2_bk0)
    x, ctx_768, mask_BxS2_bk0 = _rec_inputs()

    def _L0_xattn_setup():
        import jax, jax.numpy as jnp
        import numpy as np
        DIM_IN, DIM_LAT, DIM_HEAD = (192, 256, 64)
        INNER = max(DIM_LAT, DIM_IN)
        HEADS = INNER // DIM_HEAD
        SCALE = DIM_HEAD ** (-0.5)
        RMS_EPS = 1e-08
        LN_EPS = 1e-05

        def layernorm(x, g, b):
            mu = jnp.mean(x, axis=-1, keepdims=True)
            var = jnp.mean((x - mu) ** 2, axis=-1, keepdims=True)
            return (x - mu) * jax.lax.rsqrt(var + LN_EPS) * g + b

        def rmsnorm(x, gamma):
            norm = jnp.sqrt(jnp.sum(x * x, axis=-1, keepdims=True)) * x.shape[-1] ** (-0.5)
            return x / jnp.maximum(norm, RMS_EPS) * gamma
        key = jax.random.key(seed)
        ks = jax.random.split(key, 12)
        b, n, m = (4, 1024, 128)
        x = jax.random.normal(ks[0], (b, n, DIM_IN), jnp.float32)
        latents = jax.random.normal(ks[1], (b, m, DIM_LAT), jnp.float32)
        mask = jax.random.randint(ks[2], (b, n), 0, 2).astype(bool)
        s = lambda k, sh, fan: jax.random.normal(k, sh, jnp.float32) * fan ** (-0.5)
        return {'x': x, 'latents': latents, 'mask': mask, 'ln_x_g': jnp.ones((DIM_IN,), jnp.float32), 'ln_x_b': jnp.zeros((DIM_IN,), jnp.float32), 'ln_l_g': jnp.ones((DIM_LAT,), jnp.float32), 'ln_l_b': jnp.zeros((DIM_LAT,), jnp.float32), 'qn_g': jnp.ones((DIM_HEAD,), jnp.float32), 'kn_g': jnp.ones((DIM_HEAD,), jnp.float32), 'Wq': s(ks[3], (INNER, DIM_LAT), DIM_LAT), 'Wkv': s(ks[4], (2 * INNER, DIM_IN), DIM_IN), 'Wlkv': s(ks[5], (2 * INNER, DIM_LAT), DIM_LAT), 'Wo': s(ks[6], (DIM_LAT, INNER), INNER), 'bo': jnp.zeros((DIM_LAT,), jnp.float32)}
    _L0_xattn_all = _L0_xattn_setup()
    _L0_xattn_in = {k: v for k, v in _L0_xattn_all.items() if k in ('ln_x_g', 'ln_x_b', 'ln_l_g', 'ln_l_b', 'qn_g', 'kn_g', 'Wq', 'Wkv', 'Wlkv', 'Wo', 'bo')}
    del _L0_xattn_all

    def _L0_attn_setup():
        import jax, jax.numpy as jnp
        import numpy as np
        B, L, D, E, H = (8, 512, 256, 8, 512)

        def _reference_tuple_inner(x, Wg, bg, W1, b1, W2, b2):
            Bs, Ls, Ds = x.shape
            x_flat = x.reshape(-1, Ds)
            gate_logits = x_flat @ Wg + bg
            gate_weights = jax.nn.softmax(gate_logits, axis=-1)
            top_idx = jnp.argmax(gate_weights, axis=-1)
            top_w = jnp.max(gate_weights, axis=-1)
            hidden = jax.nn.relu(jnp.einsum('nd,edh->neh', x_flat, W1) + b1)
            expert_outputs = jnp.einsum('neh,ehd->ned', hidden, W2) + b2
            selected = jnp.take_along_axis(expert_outputs, top_idx[:, None, None], axis=1)[:, 0, :]
            out_flat = top_w[:, None] * selected
            out = out_flat.reshape(Bs, Ls, Ds)
            return (out, gate_weights)
        key = jax.random.key(seed)
        ks = jax.random.split(key, 5)
        scale_in = 1.0 / np.sqrt(D)
        scale_h = 1.0 / np.sqrt(H)
        return {'x': jax.random.normal(ks[0], (B, L, D), dtype=jnp.float32), 'Wg': jax.random.normal(ks[1], (D, E), dtype=jnp.float32) * scale_in, 'bg': jnp.zeros((E,), dtype=jnp.float32), 'W1': jax.random.normal(ks[2], (E, D, H), dtype=jnp.float32) * scale_in, 'b1': jnp.zeros((E, H), dtype=jnp.float32), 'W2': jax.random.normal(ks[3], (E, H, D), dtype=jnp.float32) * scale_h, 'b2': jnp.zeros((E, D), dtype=jnp.float32)}
    _L0_attn_all = _L0_attn_setup()
    _L0_attn_in = {k: v for k, v in _L0_attn_all.items() if k in ('Wg', 'bg', 'W1', 'b1', 'W2', 'b2')}
    del _L0_attn_all

    def _L0_ffn_setup():
        import jax, jax.numpy as jnp
        import numpy as np
        E = 8
        D = 256
        H = 512
        TOP_K = 2
        key = jax.random.key(seed)
        k_x, k_g, k_w1, k_w2 = jax.random.split(key, 4)
        B, S = (4, 512)
        inp = {'input': jax.random.normal(k_x, (B, S, D), dtype=jnp.float32), 'Wg': jax.random.normal(k_g, (D, E), dtype=jnp.float32) * 0.02, 'W1': jax.random.normal(k_w1, (E, D, H), dtype=jnp.float32) * 0.02, 'b1': jnp.zeros((E, H), dtype=jnp.float32), 'W2': jax.random.normal(k_w2, (E, H, D), dtype=jnp.float32) * 0.02, 'b2': jnp.zeros((E, D), dtype=jnp.float32)}
        return inp
    _L0_ffn_all = _L0_ffn_setup()
    _L0_ffn_in = {k: v for k, v in _L0_ffn_all.items() if k in ('Wg', 'W1', 'b1', 'W2', 'b2')}
    del _L0_ffn_all
    return {'x': x, 'ctx_768': ctx_768, 'mask_BxS2_bk0': mask_BxS2_bk0, 'L0_xattn_ln_x_g': _L0_xattn_in['ln_x_g'], 'L0_xattn_ln_x_b': _L0_xattn_in['ln_x_b'], 'L0_xattn_ln_l_g': _L0_xattn_in['ln_l_g'], 'L0_xattn_ln_l_b': _L0_xattn_in['ln_l_b'], 'L0_xattn_qn_g': _L0_xattn_in['qn_g'], 'L0_xattn_kn_g': _L0_xattn_in['kn_g'], 'L0_xattn_Wq': _L0_xattn_in['Wq'], 'L0_xattn_Wkv': _L0_xattn_in['Wkv'], 'L0_xattn_Wlkv': _L0_xattn_in['Wlkv'], 'L0_xattn_Wo': _L0_xattn_in['Wo'], 'L0_xattn_bo': _L0_xattn_in['bo'], 'L0_attn_Wg': _L0_attn_in['Wg'], 'L0_attn_bg': _L0_attn_in['bg'], 'L0_attn_W1': _L0_attn_in['W1'], 'L0_attn_b1': _L0_attn_in['b1'], 'L0_attn_W2': _L0_attn_in['W2'], 'L0_attn_b2': _L0_attn_in['b2'], 'L0_ffn_Wg': _L0_ffn_in['Wg'], 'L0_ffn_W1': _L0_ffn_in['W1'], 'L0_ffn_b1': _L0_ffn_in['b1'], 'L0_ffn_W2': _L0_ffn_in['W2'], 'L0_ffn_b2': _L0_ffn_in['b2']}

def reference(x, ctx_768, mask_BxS2_bk0, L0_xattn_ln_x_g, L0_xattn_ln_x_b, L0_xattn_ln_l_g, L0_xattn_ln_l_b, L0_xattn_qn_g, L0_xattn_kn_g, L0_xattn_Wq, L0_xattn_Wkv, L0_xattn_Wlkv, L0_xattn_Wo, L0_xattn_bo, L0_attn_Wg, L0_attn_bg, L0_attn_W1, L0_attn_b1, L0_attn_W2, L0_attn_b2, L0_ffn_Wg, L0_ffn_W1, L0_ffn_b1, L0_ffn_W2, L0_ffn_b2):
    import jax
    import jax.numpy as jnp

    def _L0_xattn_ref(x, latents, mask, ln_x_g, ln_x_b, ln_l_g, ln_l_b, qn_g, kn_g, Wq, Wkv, Wlkv, Wo, bo):
        import jax, jax.numpy as jnp
        import numpy as np
        DIM_IN, DIM_LAT, DIM_HEAD = (192, 256, 64)
        INNER = max(DIM_LAT, DIM_IN)
        HEADS = INNER // DIM_HEAD
        SCALE = DIM_HEAD ** (-0.5)
        RMS_EPS = 1e-08
        LN_EPS = 1e-05

        def layernorm(x, g, b):
            mu = jnp.mean(x, axis=-1, keepdims=True)
            var = jnp.mean((x - mu) ** 2, axis=-1, keepdims=True)
            return (x - mu) * jax.lax.rsqrt(var + LN_EPS) * g + b

        def rmsnorm(x, gamma):
            norm = jnp.sqrt(jnp.sum(x * x, axis=-1, keepdims=True)) * x.shape[-1] ** (-0.5)
            return x / jnp.maximum(norm, RMS_EPS) * gamma
        b, n, _ = x.shape
        m = latents.shape[1]
        xn = layernorm(x, ln_x_g, ln_x_b)
        ln = layernorm(latents, ln_l_g, ln_l_b)
        q = ln @ Wq.T
        kv = jnp.concatenate([xn @ Wkv.T, ln @ Wlkv.T], axis=1)
        k, v = (kv[..., :INNER], kv[..., INNER:])
        split_heads = lambda t: t.reshape(t.shape[0], t.shape[1], HEADS, DIM_HEAD).transpose(0, 2, 1, 3)
        q, k, v = (split_heads(q), split_heads(k), split_heads(v))
        qn = rmsnorm(q, qn_g) * SCALE
        kn = rmsnorm(k, kn_g)
        attn = jnp.einsum('bhid,bhjd->bhij', qn, kn)
        full_mask = jnp.pad(mask, ((0, 0), (0, m)), constant_values=True)
        attn = jnp.where(full_mask[:, None, None, :], attn, -jnp.finfo(attn.dtype).max)
        attn = jax.nn.softmax(attn, axis=-1)
        out = jnp.einsum('bhij,bhjd->bhid', attn, v)
        out = out.transpose(0, 2, 1, 3).reshape(b, m, INNER)
        return out @ Wo.T + bo

    def _L0_attn_ref(x, Wg, bg, W1, b1, W2, b2):
        import jax, jax.numpy as jnp
        import numpy as np
        B, L, D, E, H = (8, 512, 256, 8, 512)

        def _reference_tuple_inner(x, Wg, bg, W1, b1, W2, b2):
            Bs, Ls, Ds = x.shape
            x_flat = x.reshape(-1, Ds)
            gate_logits = x_flat @ Wg + bg
            gate_weights = jax.nn.softmax(gate_logits, axis=-1)
            top_idx = jnp.argmax(gate_weights, axis=-1)
            top_w = jnp.max(gate_weights, axis=-1)
            hidden = jax.nn.relu(jnp.einsum('nd,edh->neh', x_flat, W1) + b1)
            expert_outputs = jnp.einsum('neh,ehd->ned', hidden, W2) + b2
            selected = jnp.take_along_axis(expert_outputs, top_idx[:, None, None], axis=1)[:, 0, :]
            out_flat = top_w[:, None] * selected
            out = out_flat.reshape(Bs, Ls, Ds)
            return (out, gate_weights)
        return _reference_tuple_inner(x, Wg, bg, W1, b1, W2, b2)[0]

    def _L0_ffn_ref(input, Wg, W1, b1, W2, b2):
        import jax, jax.numpy as jnp
        import numpy as np
        E = 8
        D = 256
        H = 512
        TOP_K = 2
        logits = jnp.einsum('bsd,de->bse', input, Wg)
        probs = jax.nn.softmax(logits, axis=-1)
        top_vals, top_idx = jax.lax.top_k(probs, TOP_K)
        top_vals = top_vals / jnp.sum(top_vals, axis=-1, keepdims=True)
        onehot = jax.nn.one_hot(top_idx, E, dtype=input.dtype)
        mask = jnp.sum(onehot, axis=2)
        scores = jnp.sum(onehot * top_vals[..., None], axis=2)
        xm = input[None] * jnp.moveaxis(mask, -1, 0)[..., None]
        h = jnp.einsum('ebsd,edh->ebsh', xm, W1) + b1[:, None, None, :]
        h = jax.nn.relu(h)
        y = jnp.einsum('ebsh,ehd->ebsd', h, W2) + b2[:, None, None, :]
        out = jnp.sum(y * jnp.moveaxis(scores, -1, 0)[..., None], axis=0)
        return out
    x = x + _L0_xattn_ref(ctx_768, _layernorm(x, axis=-1), mask_BxS2_bk0, L0_xattn_ln_x_g, L0_xattn_ln_x_b, L0_xattn_ln_l_g, L0_xattn_ln_l_b, L0_xattn_qn_g, L0_xattn_kn_g, L0_xattn_Wq, L0_xattn_Wkv, L0_xattn_Wlkv, L0_xattn_Wo, L0_xattn_bo)
    x = x + _L0_attn_ref(_layernorm(x, axis=-1), L0_attn_Wg, L0_attn_bg, L0_attn_W1, L0_attn_b1, L0_attn_W2, L0_attn_b2)
    x = x + _L0_ffn_ref(_layernorm(x, axis=-1), L0_ffn_Wg, L0_ffn_W1, L0_ffn_b1, L0_ffn_W2, L0_ffn_b2)
    return x

_drawn_inputs = setup_inputs


def setup_inputs(seed=0):
    import zlib

    import numpy as np

    out = dict(_drawn_inputs(seed))
    spreads = {'L0_xattn_ln_x_g': (1.0, 0.2),
     'L0_xattn_ln_x_b': (0.0, 0.1),
     'L0_xattn_ln_l_g': (1.0, 0.2),
     'L0_xattn_ln_l_b': (0.0, 0.1),
     'L0_xattn_qn_g': (1.0, 0.2),
     'L0_xattn_kn_g': (1.0, 0.2),
     'L0_xattn_bo': (0.0, 0.1),
     'L0_attn_bg': (0.0, 0.1),
     'L0_attn_b1': (0.0, 0.287),
     'L0_attn_b2': (0.0, 0.1),
     'L0_ffn_b1': (0.0, 0.433),
     'L0_ffn_b2': (0.0, 0.1)}
    factors = {}
    for name, (base, spread) in spreads.items():
        noise = np.random.default_rng([zlib.crc32(name.encode()), seed]).standard_normal(out[name].shape)
        drawn = base * np.exp(spread * noise) if base else spread * noise
        out[name] = jnp.asarray(drawn.astype(out[name].dtype))
    for name, factor in factors.items():
        out[name] = (out[name] * factor).astype(out[name].dtype)
    return out
```

```python
from contextlib import ExitStack

import concourse.bass as bass
from concourse import mybir

P = 128
ALU = mybir.AluOpType
ACT = mybir.ActivationFunctionType
F32 = mybir.dt.float32
F32R = mybir.dt.float32r
U8 = mybir.dt.uint8
AX_X = mybir.AxisListType.X
ABSMAX = bass.bass_isa.ReduceOp.absmax

LN_EPS = 1e-5
RMS_FLOOR = 1e-8
MASKED = 1e30
SAFE = 60.0
RING = 4


def wait_count(eng, sem, value):
    if isinstance(value, int) and value <= 0:
        return
    eng.wait_ge(sem, value)


def run_steps(eng, step, first, loop_first, loop_end, last):
    for s in range(first, loop_first):
        step(s, s)
    with eng.Fori(0, (loop_end - loop_first) // RING) as turn:
        for u in range(RING):
            step(turn * RING + (loop_first + u), loop_first + u)
    for s in range(loop_end, last + 1):
        step(s, s)


def perceiver_block(nc, t, out):
    NCTX, DC = t["ctx_768"].shape[1:]
    _, NL, DL = t["x"].shape
    DH = 64
    H = DL // DH
    E, _, HID = t["L0_attn_W1"].shape
    NT = NCTX // P
    NP = NT // 2
    CX = DC - P
    ONE = DC - 1
    CL = DL // P
    HC = HID // P
    SCALE = float(DH) ** -0.5
    assert NL == P and DL == 2 * P and NT == 2 * NP and H * NL == 512 and CX == P // 2

    FIRST, LAST = -2, NP - 1 + 3
    LOOP_FIRST = 4
    LOOP_END = LOOP_FIRST + (NP - 2 - LOOP_FIRST) // RING * RING

    with ExitStack() as ctx:
        def sb(name, shape, dt=F32):
            return ctx.enter_context(nc.sbuf_tensor(name, shape, dt))

        def sem(name):
            return ctx.enter_context(nc.semaphore(name))

        bank = [ctx.enter_context(nc.psum_tensor(f"bank{i}", [P, 512], F32)) for i in range(8)]

        w1 = [sb(f"w1_{l}", [P, E * CL, HID]) for l in range(2)]
        w2 = [sb(f"w2_{l}", [P, E * HC, DL]) for l in range(2)]
        prep_area = w2[1][:].rearrange("p a n -> p (a n)")
        prep_used = [0]

        def prep(a, n):
            at = prep_used[0]
            prep_used[0] = at + a * n
            assert prep_used[0] <= E * HC * DL
            return prep_area[:, at:at + a * n].rearrange("p (a n) -> p a n", a=a)

        ident = sb("ident", [P, P])
        ones_row = sb("ones_row", [1, P])
        minus_half = sb("minus_half", [P, 16])
        rank = sb("rank", [P, E])
        cols = sb("cols", [P, t["columns"].shape[1]])
        at = iter(range(cols.shape[1]))

        def column(n=1):
            first = next(at)
            for _ in range(n - 1):
                next(at)
            return cols[:, first:first + n]

        ln_l_g, ln_l_b = column(CL), column(CL)
        ln_x_g, ln_x_b = column(2), column(2)
        qn_g, kn_g = column(), column()
        wg = [column(CL * E).rearrange("p (c e) -> p c e", c=CL) for _ in range(2)]
        b1T = [column(E * HC) for _ in range(2)]
        bo_row = sb("bo_row", [1, DL])
        bg_row = sb("bg_row", [1, E])
        mask_u8 = sb("mask_u8", [P, NT], U8)
        b2 = [sb(f"b2_{l}", [E, DL]) for l in range(2)]

        x_nat = sb("x_nat", [P, DL])
        woT = sb("woT", [P, CL, DL])
        wqT = prep(CL, DL)
        wlkvT = prep(CL, 2 * DL)
        wkvT = prep(2, 2 * DL)
        wk = prep(2, DL)
        last_row = prep(1, P)[0:CX, 0]
        g_last = prep(1, P)[0:CX, 0]
        b_one = prep(2, P)
        one_col = sb("one_col", [P, 1])
        g_col = sb("g_col", [P, 2])
        b_neg = sb("b_neg", [P, 2])
        wk_hi = sb("wk_hi", [P, 2, DL], F32R)
        wk_lo = sb("wk_lo", [P, 2, DL], F32R)
        wv = sb("wv", [P, 2, H, DH + 1])

        lat = [sb(f"lat{n}", [P, DL]) for n in range(2)]
        stats = sb("stats", [P, 6])
        mean_var = sb("mean_var", [P, 2])
        pow_in = sb("pow_in", [P, 2 * H])
        pow_out = sb("pow_out", [P, 2 * H])
        latT = sb("latT", [P, CL, P])
        qk = prep(2, DL)
        qk_sq = prep(2, DL)
        v_own = sb("v_own", [P, H, DH + 1])
        q_gain = sb("q_gain", [P, 2])
        amax = sb("amax", [P, 1])
        shift = sb("shift", [P, 2])
        mask_f = sb("mask_f", [P, NT])
        bias = sb("bias", [P, NT])
        q_bd = prep(2, 2 * P)
        q_hi = sb("q_hi", [P, 2, 2 * P], F32R)
        q_lo = sb("q_lo", [P, 2, 2 * P], F32R)
        e_own = sb("e_own", [P, 512])

        x_in = sb("x_in", [P, RING, 2, DC])
        xh = sb("xh", [P, 2, 2, ONE])
        x_hl = sb("x_hl", [P, RING, 2, 2 * DC], F32R)
        A_HI, B_HL, A_LO = slice(0, P), slice(P, P + 2 * CX), slice(DC + CX, 2 * DC)
        x_stats = sb("x_stats", [P, 2, 6])
        x_mv = sb("x_mv", [P, RING, 2, 2])
        x_var = sb("x_var", [P, 2, 2])
        x_rstd = sb("x_rstd", [P, 2, 2])
        k_ms = sb("k_ms", [P, 2 * H])
        k_rs = sb("k_rs", [P, 2 * H])
        xT = sb("xT", [P, 2, 2, P], F32R)
        xT_lo = sb("xT_lo", [P, 2, P], F32R)
        k_sb = sb("k_sb", [P, 2, 2 * DL])
        k_sq = sb("k_sq", [P, 2 * DL])
        k_ss = sb("k_ss", [P, 2 * H])
        kn = sb("kn", [P, 2, 2, P])
        kT_hi = sb("kT_hi", [P, 2, 2, P], F32R)
        kT_lo = sb("kT_lo", [P, 2, 2, P], F32R)
        e_f32 = sb("e_f32", [P, 2, 512])
        e_hi = sb("e_hi", [P, 2, 512], F32R)
        e_lo = sb("e_lo", [P, 2, 512], F32R)

        uT = k_sb
        den_r = sb("den_r", [P, H])
        o_sb = sb("o_sb", [P, DL])
        oT = sb("oT", [P, CL, P])
        x_cur = [sb(f"x_cur{l}", [P, DL]) for l in range(3)]
        g_max = sb("g_max", [P, 4])
        g_e = sb("g_e", [P, E])
        g_p = sb("g_p", [P, 8, E])
        wgt = sb("wgt", [P, E])
        wgtT = sb("wgtT", [E, P])
        hT = e_f32[:].rearrange("p a (c n) -> p a c n", c=HC)

        U_BANK = [bank[0], bank[1]]
        XT_BANK, K_BANK, KT_BANK = bank[2], bank[3], bank[4]
        S_BANK = [bank[5], bank[6]]

        consts_ready = sem("consts_ready")
        zeros_ready = sem("zeros_ready")
        small_loaded = sem("small_loaded")
        x_nat_loaded = sem("x_nat_loaded")
        w_loaded = {n: sem(f"{n}_loaded") for n in ("wqT", "wkvT", "wlkvT", "woT")}
        cols_loaded = sem("cols_loaded")
        experts_loaded = [sem(f"experts_loaded{l}") for l in range(2)]
        last_gain_ready = sem("last_gain_ready")
        taken_off_in_psum = sem("taken_off_in_psum")
        dve_step = sem("dve_step")
        var_ready = sem("var_ready")
        rstd_ready = sem("rstd_ready")
        lat_ready = sem("lat_ready")
        latT_in_psum = sem("latT_in_psum")
        latT_ready = sem("latT_ready")
        qkv_in_psum = sem("qkv_in_psum")
        qk_ready = sem("qk_ready")
        v_own_ready = sem("v_own_ready")
        qk_normed = sem("qk_normed")
        qkT_in_psum = sem("qkT_in_psum")
        gain_ready = sem("gain_ready")
        amax_ready = sem("amax_ready")
        bias_ready = sem("bias_ready")
        q_split = sem("q_split")
        own_kT_hi = sem("own_kT_hi")
        own_kT_split = sem("own_kT_split")
        own_scores = sem("own_scores")
        own_probs = sem("own_probs")
        prep_done = sem("prep_done")

        x_loaded = [sem(f"x_loaded{k}") for k in range(RING)]
        x_hi_ready = sem("x_hi_ready")
        x_split = sem("x_split")
        x_stats_ready = sem("x_stats_ready")
        x_mv_ready = sem("x_mv_ready")
        k_summed = sem("k_summed")
        k_ms_ready = sem("k_ms_ready")
        k_rs_ready = sem("k_rs_ready")
        x_var_ready = sem("x_var_ready")
        x_rstd_ready = sem("x_rstd_ready")
        xh_ready = sem("xh_ready")
        xT_in_psum = sem("xT_in_psum")
        xT_ready = sem("xT_ready")
        xT_split = sem("xT_split")
        k_in_psum = sem("k_in_psum")
        k_in_sbuf = sem("k_in_sbuf")
        k_squared = sem("k_squared")
        kn_ready = sem("kn_ready")
        kT_in_psum = sem("kT_in_psum")
        kT_hi_ready = sem("kT_hi_ready")
        kT_split = sem("kT_split")
        scores_ready = sem("scores_ready")
        probs_ready = sem("probs_ready")
        e_hi_ready = sem("e_hi_ready")
        e_split = sem("e_split")
        probs_used = sem("probs_used")

        uT_ready = sem("uT_ready")
        heads_in_psum = sem("heads_in_psum")
        o_ready = sem("o_ready")
        oT_in_psum = sem("oT_in_psum")
        oT_ready = sem("oT_ready")
        attn_in_psum = sem("attn_in_psum")
        xn_ready = sem("xn_ready")
        xnT_in_psum = sem("xnT_in_psum")
        xnT_ready = sem("xnT_ready")
        logits_in_psum = sem("logits_in_psum")
        logits_max = sem("logits_max")
        gate_exp = sem("gate_exp")
        wgt_ready = sem("wgt_ready")
        wgtT_in_psum = sem("wgtT_in_psum")
        wgtT_ready = sem("wgtT_ready")
        b2_in_psum = sem("b2_in_psum")
        h_in_psum = sem("h_in_psum")
        h_ready = sem("h_ready")
        y_in_psum = sem("y_in_psum")
        y_added = sem("y_added")
        out_ready = sem("out_ready")
        out_stored = sem("out_stored")

        ctx_rows = t["ctx_768"][0].rearrange("(p a j) d -> a p j d", p=P, j=2)
        SMALL = 5

        block = ctx.enter_context(nc.Block())

        @block.sync
        def _(sp):
            sp.dma_start(x_nat[:], t["x"][0]).then_inc(x_nat_loaded, 16)
            sp.dma_start(wkvT[:], t["wkvT"].rearrange("c p n -> p c n")).then_inc(w_loaded["wkvT"], 16)
            sp.dma_start(wlkvT[:], t["wlkvT"].rearrange("(c p) n -> p c n", p=P)).then_inc(w_loaded["wlkvT"], 16)

            def load(i, r):
                wait_count(sp, xh_ready, i - RING + 1)
                sp.dma_start(x_in[:, r % RING], ctx_rows[bass.ds(i, 1)].rearrange("a p j d -> (a p) j d")
                             if not isinstance(i, int) else ctx_rows[i]).then_inc(x_loaded[r % RING], 16)

            run_steps(sp, load, 0, RING, RING + (NP - RING) // RING * RING, NP - 1)
            sp.wait_ge(out_ready, 1)
            sp.dma_start(out[0], x_cur[2][:]).then_inc(out_stored, 16)
            sp.wait_ge(out_stored, 16)

        @block.gpsimd
        def _(gp):
            gp.memset(ident[:], 0.0).then_inc(zeros_ready, 1)
            gp.memset(last_row, 0.0).then_inc(zeros_ready, 1)
            gp.memset(minus_half[:], -0.5).then_inc(consts_ready, 1)
            gp.memset(ones_row[:], 1.0).then_inc(consts_ready, 1)
            gp.wait_ge(zeros_ready, 2)
            gp.affine_select(out=ident[:], in_=ident[:], compare_op=ALU.not_equal, fill=1.0, base=0,
                             pattern=[[-1, P]], channel_multiplier=1).then_inc(consts_ready, 1)
            gp.affine_select(out=last_row, in_=last_row, compare_op=ALU.not_equal, fill=1.0, base=1 - CX,
                             pattern=[[0, P]], channel_multiplier=1).then_inc(consts_ready, 1)
            gp.iota(rank[:], [[-1, E]], base=E, channel_multiplier=0,
                    allow_small_or_imprecise_dtypes=True).then_inc(consts_ready, 1)

            def power(n, cols):
                gp.wait_ge(var_ready, n)
                gp.tensor_tensor(pow_out[:, 0:cols], pow_in[:, 0:cols], minus_half[:, 0:cols], ALU.pow).then_inc(rstd_ready, 1)

            gp.wait_ge(consts_ready, 5)
            power(1, 1)
            power(2, 1)
            gp.wait_ge(gain_ready, 1)
            gp.partition_all_reduce(amax[:], q_gain[:, 0:1], P, ABSMAX).then_inc(amax_ready, 1)

            def step(s, r):
                if 0 <= r + 1 < NP:
                    gp.wait_ge(x_var_ready, s + 1 + 1)
                    gp.tensor_tensor(x_rstd[:, (r + 1) % 2], x_var[:, (r + 1) % 2], minus_half[:, 0:2], ALU.pow).then_inc(x_rstd_ready, 1)
                if 0 <= r - 1 < NP:
                    i = s - 1
                    gp.wait_ge(k_ms_ready, i + 1)
                    wait_count(gp, kn_ready, i)
                    gp.tensor_tensor(k_rs[:], k_ms[:], minus_half[:, 0:2 * H], ALU.pow).then_inc(k_rs_ready, 1)
                    gp.wait_ge(k_in_sbuf, i + 1)
                    gp.wait_ge(k_rs_ready, i + 1)
                    wait_count(gp, kT_in_psum, i)
                    gp.tensor_tensor(kn[:].rearrange("p j c (g d) -> p (j c g) d", d=DH),
                                     k_sb[:, (r - 1) % 2].rearrange("p (g d) -> p g d", d=DH),
                                     k_rs[:].unsqueeze(2).broadcast_to([P, 2 * H, DH]),
                                     ALU.mult).then_inc(kn_ready, 1)
                if 0 <= r + 1 < NP:
                    i = s + 1
                    gp.wait_ge(x_hi_ready, i + 1)
                    both = x_hl[:, (r + 1) % RING]
                    gp.tensor_tensor(both[:, :, A_LO], xh[:, (r + 1) % 2, :, 0:P], both[:, :, A_HI].bitcast(F32), ALU.subtract)
                    gp.tensor_tensor(both[:, :, DC:DC + CX - 1], xh[:, (r + 1) % 2, :, P:ONE],
                                     both[:, :, P:ONE].bitcast(F32), ALU.subtract).then_inc(x_split, 1)

            step(-2, -2)
            step(-1, -1)
            power(3, 2 * H)
            run_steps(gp, step, 0, LOOP_FIRST, LOOP_END, LAST)
            power(4, 1)
            power(5, 1)

        @block.scalar
        def _(act):
            act.dma_start(cols[:], t["columns"]).then_inc(cols_loaded, 16)
            act.dma_start(wqT[:], t["wqT"].rearrange("(c p) n -> p c n", p=P)).then_inc(w_loaded["wqT"], 16)
            act.dma_start(mask_u8[:], t["mask_BxS2_bk0"][0].rearrange("(p a) -> p a", p=P)).then_inc(small_loaded, 16)
            act.dma_start(bo_row[:], t["L0_xattn_bo"].rearrange("(a n) -> a n", a=1)).then_inc(small_loaded, 16)
            act.dma_start(bg_row[:], t["L0_attn_bg"].rearrange("(a n) -> a n", a=1)).then_inc(small_loaded, 16)
            for l, n in enumerate(("attn", "ffn")):
                act.dma_start(b2[l][:], t[f"L0_{n}_b2"]).then_inc(small_loaded, 16)
            act.dma_start(woT[:], t["woT"].rearrange("(c p) n -> p c n", p=P)).then_inc(w_loaded["woT"], 16)

            def load_experts(l, src, dst):
                rows = src.rearrange("e k n -> (e k) n").rearrange("(a p) n -> p a n", p=P)
                k = rows.shape[1] // 4
                for q in range(4):
                    act.dma_start(dst[:, q * k:(q + 1) * k], rows[:, q * k:(q + 1) * k]).then_inc(experts_loaded[l], 16)

            def split_probs(i, j):
                act.wait_ge(probs_ready, 2 * i + j + 1)
                wait_count(act, probs_used, 2 * (i - 1) + j + 1)
                act.activation(e_hi[:, j], e_f32[:, j], ACT.Copy).then_inc(e_hi_ready, 1)

            def exponentials(i, j):
                act.wait_ge(scores_ready, 2 * i + j + 1)
                wait_count(act, e_split, 2 * (i - 1) + j + 1)
                tile = 2 * i + j
                b = bias[:, tile:tile + 1] if isinstance(i, int) else bias[:, bass.ds(tile, 1)]
                act.activation(e_f32[:, j], S_BANK[j][:], ACT.Exp, bias=b).then_inc(probs_ready, 1)

            def step(s, r):
                if 0 <= r - 1 < NP:
                    i = s - 1
                    act.wait_ge(k_in_psum, i + 1)
                    wait_count(act, k_summed, i)
                    act.activation(k_sq[:], K_BANK[:], ACT.Square).then_inc(k_squared, 1)
                if 0 <= r - 3 < NP:
                    split_probs(s - 3, 1)
                if 0 <= r - 2 < NP:
                    i = s - 2
                    act.wait_ge(kT_in_psum, i + 1)
                    wait_count(act, scores_ready, 2 * i)
                    act.activation(kT_hi[:].rearrange("p j c n -> p (j c n)"), KT_BANK[:], ACT.Copy).then_inc(kT_hi_ready, 1)
                if 0 <= r - 1 < NP:
                    i = s - 1
                    wait_count(act, kn_ready, i - 1)
                    act.activation(k_sb[:, (r - 1) % 2], K_BANK[:], ACT.Copy).then_inc(k_in_sbuf, 1)
                if 0 <= r < NP:
                    act.wait_ge(xT_in_psum, s + 1)
                    wait_count(act, k_in_psum, s)
                    act.activation(xT[:].rearrange("p j c n -> p (j c n)"), XT_BANK[:], ACT.Copy).then_inc(xT_ready, 1)
                if 0 <= r + 1 < NP:
                    i = s + 1
                    act.wait_ge(xh_ready, i + 1)
                    wait_count(act, probs_used, 2 * (i - RING) + 2)
                    act.activation(x_hl[:, (r + 1) % RING, :, 0:ONE], xh[:, (r + 1) % 2], ACT.Copy).then_inc(x_hi_ready, 1)
                if 0 <= r - 2 < NP:
                    exponentials(s - 2, 0)
                    split_probs(s - 2, 0)
                    exponentials(s - 2, 1)

            step(-2, -2)
            step(-1, -1)
            act.wait_ge(qkv_in_psum, 1)
            act.activation(qk[:, 0], bank[1][:, 0:DL], ACT.Copy).then_inc(qk_ready, 1)
            act.wait_ge(qkv_in_psum, 2)
            act.activation(qk[:, 1], bank[7][:, 0:DL], ACT.Copy).then_inc(qk_ready, 1)
            act.activation(v_own[:, :, 0:DH], bank[7][:, DL:2 * DL].rearrange("p (h d) -> p h d", d=DH),
                           ACT.Copy).then_inc(v_own_ready, 1)
            load_experts(0, t["L0_attn_W1"], w1[0])
            load_experts(0, t["L0_attn_W2"], w2[0])
            load_experts(1, t["L0_ffn_W1"], w1[1])
            step(0, 0)
            act.wait_ge(qkT_in_psum, 2)
            act.activation(kT_hi[:, 0], bank[6][:, 0:2 * P].rearrange("p (c n) -> p c n", c=2), ACT.Copy).then_inc(own_kT_hi, 1)
            step(1, 1)
            act.wait_ge(own_scores, 1)
            act.wait_ge(bias_ready, 1)
            act.activation(e_own[:], S_BANK[0][:], ACT.Exp, bias=shift[:, 1:2]).then_inc(own_probs, 1)
            act.wait_ge(prep_done, 1)
            load_experts(1, t["L0_ffn_W2"], w2[1])
            run_steps(act, step, 2, LOOP_FIRST, LOOP_END, LAST)

            act.wait_ge(probs_used, 2 * NP)
            act.activation(uT[:, 0], U_BANK[0][:], ACT.Copy).then_inc(uT_ready, 1)
            act.wait_ge(oT_in_psum, 1)
            act.activation(oT[:].rearrange("p c n -> p (c n)"), bank[2][:, 0:DL], ACT.Copy).then_inc(oT_ready, 1)
            for l in range(2):
                act.wait_ge(xnT_in_psum, l + 1)
                act.activation(latT[:].rearrange("p c n -> p (c n)"), bank[2][:, 0:DL], ACT.Copy).then_inc(xnT_ready, 1)
                act.wait_ge(logits_max, l + 1)
                act.activation(g_e[:], bank[3][:, 0:E], ACT.Exp, bias=g_max[:, 0:1]).then_inc(gate_exp, 1)
                for e in range(E):
                    n = l * E + e
                    act.wait_ge(h_in_psum, n + 1)
                    wait_count(act, y_in_psum, n - 1)
                    for c in range(HC):
                        last = act.activation(hT[:, n % 2, c], bank[6 + n % 2][:, c * P:(c + 1) * P], ACT.Relu,
                                              bias=b1T[l][:, e * HC + c:e * HC + c + 1])
                    last.then_inc(h_ready, 1)

        @block.vector
        def _(dve):
            chain = [0]

            def link(ins):
                chain[0] += 1
                ins.then_inc(dve_step, 1)
                dve.wait_ge(dve_step, chain[0])

            def norm(n, dst, src):
                link(dve.bn_stats(stats[:], src))
                link(dve.bn_aggr(mean_var[:], stats[:]))
                dve.tensor_scalar(pow_in[:, 0:1], mean_var[:, 1:2], LN_EPS, None, ALU.add).then_inc(var_ready, 1)
                dve.wait_ge(rstd_ready, n)
                return dve.tensor_scalar(dst, src, mean_var[:, 0:1], pow_out[:, 0:1], ALU.subtract, ALU.mult)

            def slot_loads(i, r):
                if isinstance(i, int):
                    return 16 * (i // RING + 1)
                return (i - r % RING) * (16 // RING) + 16

            def split_probs(s, j):
                n = 2 * (s - 3) + j + 1
                dve.wait_ge(e_hi_ready, n)
                wait_count(dve, probs_used, n - 2)
                dve.tensor_tensor(e_lo[:, j], e_f32[:, j], e_hi[:, j].bitcast(F32), ALU.subtract).then_inc(e_split, 1)

            def step(s, r):
                if 0 <= r - 3 < NP:
                    split_probs(s, 0)
                if 0 <= r + 1 < NP:
                    i, slot = s + 1, (r + 1) % RING
                    dve.wait_ge(x_rstd_ready, i + 1)
                    wait_count(dve, x_split, i - 1)
                    wait_count(dve, xT_in_psum, i - 1)
                    for j in range(2):
                        last = dve.tensor_scalar(xh[:, (r + 1) % 2, j], x_in[:, slot, j, 0:ONE], x_mv[:, slot, j, 0:1],
                                                 x_rstd[:, (r + 1) % 2, j:j + 1], ALU.subtract, ALU.mult)
                    last.then_inc(xh_ready, 1)
                if 0 <= r - 1 < NP:
                    i = s - 1
                    dve.wait_ge(k_squared, i + 1)
                    dve.tensor_reduce(k_ss[:], k_sq[:].rearrange("p (g d) -> p g d", d=DH), AX_X, ALU.add).then_inc(k_summed, 1)
                    dve.wait_ge(k_summed, i + 1)
                    wait_count(dve, k_rs_ready, i)
                    dve.tensor_scalar(k_ms[:], k_ss[:], 1.0 / DH, RMS_FLOOR ** 2, ALU.mult, ALU.max).then_inc(k_ms_ready, 1)
                if 0 <= r - 3 < NP:
                    split_probs(s, 1)
                if 0 <= r - 2 < NP:
                    dve.wait_ge(kT_hi_ready, s - 2 + 1)
                    dve.tensor_tensor(kT_lo[:].rearrange("p j c n -> p (j c n)"), KT_BANK[:],
                                      kT_hi[:].rearrange("p j c n -> p (j c n)").bitcast(F32), ALU.subtract).then_inc(kT_split, 1)
                if r + 2 < NP:
                    i, slot = s + 2, (r + 2) % RING
                    dve.wait_ge(x_loaded[slot], slot_loads(i, r + 2))
                    for j in range(2):
                        last = dve.bn_stats(x_stats[:, j], x_in[:, slot, j])
                    last.then_inc(x_stats_ready, 1)
                    dve.wait_ge(x_stats_ready, i + 1)
                if 0 <= r < NP:
                    dve.wait_ge(xT_ready, s + 1)
                    dve.tensor_tensor(xT_lo[:], XT_BANK[:].rearrange("p (j c n) -> p j c n", j=2, c=2)[:, :, 0],
                                      xT[:, :, 0].bitcast(F32), ALU.subtract).then_inc(xT_split, 1)
                if r + 2 < NP:
                    for j in range(2):
                        last = dve.bn_aggr(x_mv[:, slot, j], x_stats[:, j])
                    last.then_inc(x_mv_ready, 1)
                    dve.wait_ge(x_mv_ready, i + 1)
                    dve.tensor_scalar(x_var[:, r % 2], x_mv[:, slot, :, 1], LN_EPS, None, ALU.add).then_inc(x_var_ready, 1)

            dve.memset(q_bd[:], 0.0)
            dve.memset(b_one[:], 0.0)
            dve.memset(v_own[:, :, DH:DH + 1], 1.0).then_inc(v_own_ready, 1)
            dve.memset(x_hl[:, :, :, DC + CX - 1:DC + CX].bitcast(F32), 0.0)
            dve.memset(wv[:, 0, :, DH:DH + 1], 0.0)
            link(dve.memset(x_hl[:, :, :, ONE:DC].bitcast(F32), 1.0))
            dve.wait_ge(x_nat_loaded, 16)
            link(norm(1, lat[0][:], x_nat[:]))
            norm(2, lat[1][:], lat[0][:]).then_inc(lat_ready, 1)
            dve.wait_ge(consts_ready, 5)
            link(dve.tensor_tensor(one_col[:], ident[:, CX - 1:CX], ident[:, P - 1:P], ALU.add))
            dve.wait_ge(cols_loaded, 16)
            link(dve.tensor_tensor(q_gain[:, 0:1], qn_g, kn_g, ALU.mult))
            dve.tensor_scalar(q_gain[:, 1:2], q_gain[:, 0:1], SCALE, None, ALU.mult).then_inc(gain_ready, 1)
            dve.tensor_scalar(g_last, last_row, ln_x_g[0:CX, 1:2], None, ALU.mult)
            dve.tensor_scalar(b_one[0:CX, 1], last_row, ln_x_g[0:CX, 1:2], None, ALU.mult)
            link(dve.tensor_scalar(b_neg[:], ln_x_b, -1.0, None, ALU.mult))
            dve.tensor_copy(b_one[:, 0, CX - 1::CX], b_neg[:, 0:1].broadcast_to([P, 2]))
            dve.tensor_copy(b_one[0:CX, 1, CX - 1::CX], b_neg[0:CX, 1:2].broadcast_to([CX, 2])).then_inc(last_gain_ready, 1)
            dve.tensor_copy(g_col[:, 0:1], ln_x_g[:, 0:1])
            dve.tensor_tensor(g_col[:, 1:2], one_col[:], ln_x_g[:, 1:2], ALU.mult)
            link(dve.tensor_copy(wv[:, 1, :, DH], one_col[:].broadcast_to([P, H])))
            link(dve.tensor_tensor(g_col[:, 1:2], ln_x_g[:, 1:2], g_col[:, 1:2], ALU.subtract))
            dve.wait_ge(latT_in_psum, 1)
            for c in range(CL):
                last = dve.tensor_scalar(latT[:, c], bank[0][:, c * P:(c + 1) * P], ln_l_g[:, c:c + 1],
                                         ln_l_b[:, c:c + 1], ALU.mult, ALU.add)
            last.then_inc(latT_ready, 1)
            step(-2, -2)
            dve.wait_ge(taken_off_in_psum, 1)
            for c in range(2):
                dve.scalar_tensor_tensor(out=wk[:, c], in0=wkvT[:, c, 0:DL], scalar=g_col[:, c:c + 1],
                                         in1=bank[5 + c][:, 0:DL], op0=ALU.mult, op1=ALU.subtract)
                last = dve.scalar_tensor_tensor(out=wv[:, c, :, 0:DH], in0=wkvT[:, c, DL:2 * DL].rearrange("p (h d) -> p h d", d=DH),
                                                scalar=g_col[:, c:c + 1],
                                                in1=bank[5 + c][:, DL:2 * DL].rearrange("p (h d) -> p h d", d=DH),
                                                op0=ALU.mult, op1=ALU.subtract)
            link(last)
            link(dve.tensor_copy(wk_hi[:], wk[:]))
            dve.tensor_tensor(wk_lo[:], wk[:], wk_hi[:].bitcast(F32), ALU.subtract).then_inc(prep_done, 1)
            step(-1, -1)
            dve.wait_ge(qk_ready, 2)
            link(dve.tensor_tensor(qk_sq[:], qk[:], qk[:], ALU.mult))
            link(dve.tensor_reduce(pow_in[:], qk_sq[:].rearrange("p a (h d) -> p (a h) d", d=DH), AX_X, ALU.add))
            dve.tensor_scalar(pow_in[:], pow_in[:], 1.0 / DH, RMS_FLOOR ** 2, ALU.mult, ALU.max).then_inc(var_ready, 1)
            step(0, 0)
            dve.wait_ge(rstd_ready, 3)
            dve.tensor_tensor(qk[:].rearrange("p a (h d) -> p (a h) d", d=DH), qk[:].rearrange("p a (h d) -> p (a h) d", d=DH),
                              pow_out[:].unsqueeze(2).broadcast_to([P, 2 * H, DH]), ALU.mult).then_inc(qk_normed, 1)
            dve.wait_ge(amax_ready, 1)
            link(dve.tensor_scalar(shift[:, 0:1], amax[:], -SCALE * DH, SAFE, ALU.mult, ALU.add))
            link(dve.tensor_scalar(shift[:, 1:2], shift[:, 0:1], 0.0, None, ALU.min))
            dve.wait_ge(small_loaded, 16 * SMALL)
            link(dve.tensor_scalar(mask_f[:], mask_u8[:], MASKED, -MASKED, ALU.mult, ALU.add))
            dve.tensor_scalar(bias[:], mask_f[:], shift[:, 1:2], None, ALU.add).then_inc(bias_ready, 1)
            dve.wait_ge(qkT_in_psum, 1)
            for half in range(2):
                rows = slice(half * DH, (half + 1) * DH)
                last = dve.tensor_scalar(q_bd[rows, :, half * P:(half + 1) * P],
                                         bank[5][rows, 0:2 * P].rearrange("p (c n) -> p c n", c=2),
                                         q_gain[rows, 1:2], None, ALU.mult)
            link(last)
            link(dve.tensor_copy(q_hi[:], q_bd[:]))
            dve.tensor_tensor(q_lo[:], q_bd[:], q_hi[:].bitcast(F32), ALU.subtract).then_inc(q_split, 1)
            dve.wait_ge(own_kT_hi, 1)
            dve.tensor_tensor(kT_lo[:, 0], bank[6][:, 0:2 * P].rearrange("p (c n) -> p c n", c=2),
                              kT_hi[:, 0].bitcast(F32), ALU.subtract).then_inc(own_kT_split, 1)

            run_steps(dve, step, 1, LOOP_FIRST, LOOP_END, LAST)

            dve.wait_ge(probs_used, 2 * NP)
            dve.tensor_copy(uT[:, 1], U_BANK[1][:]).then_inc(uT_ready, 1)
            dve.wait_ge(heads_in_psum, 1)
            heads = bank[7][:, 0:H * (DH + 1)].rearrange("p (h d) -> p h d", d=DH + 1)
            link(dve.reciprocal(den_r[:], heads[:, :, DH]))
            dve.tensor_tensor(o_sb[:].rearrange("p (h d) -> p h d", d=DH), heads[:, :, 0:DH],
                              den_r[:].unsqueeze(2).broadcast_to([P, H, DH]), ALU.mult).then_inc(o_ready, 1)
            dve.wait_ge(attn_in_psum, 1)
            link(dve.tensor_tensor(x_cur[0][:], bank[4][:, 0:DL], x_nat[:], ALU.add))

            for l in range(2):
                norm(3 + l + 1, lat[0][:], x_cur[l][:]).then_inc(xn_ready, 1)
                p, cand, first, rest, cand2, second, w_a, w_b = (g_p[:, k] for k in range(8))
                dve.wait_ge(logits_in_psum, l + 1)
                dve.tensor_reduce(g_max[:, 0:1], bank[3][:, 0:E], AX_X, ALU.max, negate=True).then_inc(logits_max, 1)
                dve.wait_ge(gate_exp, l + 1)
                link(dve.tensor_reduce(g_max[:, 1:2], g_e[:], AX_X, ALU.add))
                link(dve.reciprocal(g_max[:, 2:3], g_max[:, 1:2]))
                link(dve.tensor_scalar(p, g_e[:], g_max[:, 2:3], None, ALU.mult))
                link(dve.tensor_reduce(g_max[:, 0:1], p, AX_X, ALU.max))
                link(dve.scalar_tensor_tensor(out=cand, in0=p, scalar=g_max[:, 0:1], in1=rank[:], op0=ALU.is_equal, op1=ALU.mult))
                link(dve.tensor_reduce(g_max[:, 1:2], cand, AX_X, ALU.max))
                link(dve.tensor_scalar(first, cand, g_max[:, 1:2], None, ALU.is_equal))
                if l == 0:
                    dve.tensor_tensor(wgt[:], first, p, ALU.mult).then_inc(wgt_ready, 1)
                else:
                    link(dve.scalar_tensor_tensor(out=rest, in0=first, scalar=-2.0, in1=p, op0=ALU.mult, op1=ALU.add))
                    link(dve.tensor_reduce(g_max[:, 1:2], rest, AX_X, ALU.max))
                    link(dve.scalar_tensor_tensor(out=cand2, in0=rest, scalar=g_max[:, 1:2], in1=rank[:], op0=ALU.is_equal, op1=ALU.mult))
                    link(dve.tensor_reduce(g_max[:, 2:3], cand2, AX_X, ALU.max))
                    link(dve.tensor_scalar(second, cand2, g_max[:, 2:3], None, ALU.is_equal))
                    link(dve.tensor_tensor(w_a, first, second, ALU.add))
                    link(dve.tensor_tensor(w_b, w_a, p, ALU.mult))
                    link(dve.tensor_tensor(g_max[:, 3:4], g_max[:, 0:1], g_max[:, 1:2], ALU.add))
                    link(dve.reciprocal(g_max[:, 2:3], g_max[:, 3:4]))
                    dve.tensor_scalar(wgt[:], w_b, g_max[:, 2:3], None, ALU.mult).then_inc(wgt_ready, 1)
                dve.wait_ge(wgtT_in_psum, l + 1)
                dve.tensor_copy(wgtT[:], bank[4][0:E, 0:P]).then_inc(wgtT_ready, 1)
                dve.wait_ge(b2_in_psum, l + 1)
                link(dve.tensor_tensor(x_cur[l + 1][:], bank[5][:, 0:DL], x_cur[l][:], ALU.add))
                for e in range(E):
                    n = l * E + e
                    dve.wait_ge(y_in_psum, n + 1)
                    last = dve.scalar_tensor_tensor(out=x_cur[l + 1][:], in0=bank[n % 2][:, 0:DL], scalar=wgt[:, e:e + 1],
                                                    in1=x_cur[l + 1][:], op0=ALU.mult, op1=ALU.add)
                    last.then_inc(y_added, 1)
                    dve.wait_ge(y_added, n + 1)
            dve.tensor_copy(x_cur[0][0:1, 0:1], x_cur[2][0:1, 0:1]).then_inc(out_ready, 1)

        @block.tensor
        def _(pe):
            def turn(dst, src):
                return pe.transpose(dst, src, ident[0:src.shape[0], 0:src.shape[0]])

            pe.wait_ge(consts_ready, 5)
            pe.wait_ge(lat_ready, 1)
            for c in range(CL):
                last = turn(bank[0][:, c * P:(c + 1) * P], lat[1][:, c * P:(c + 1) * P])
            last.then_inc(latT_in_psum, 1)
            pe.wait_ge(w_loaded["wkvT"], 16)
            pe.wait_ge(last_gain_ready, 1)
            pe.matmul(bank[5][:], g_last, wkvT[0:CX, 1], start=True, stop=True)
            pe.matmul(bank[6][:], b_one[:, 0], wkvT[:, 0], start=True, stop=False)
            pe.matmul(bank[6][:], b_one[0:CX, 1], wkvT[0:CX, 1], start=False, stop=True).then_inc(taken_off_in_psum, 1)
            pe.wait_ge(latT_ready, 1)
            pe.wait_ge(w_loaded["wqT"], 16)
            for c in range(CL):
                last = pe.matmul(bank[1][:, 0:DL], latT[:, c], wqT[:, c], start=(c == 0), stop=(c == CL - 1))
            last.then_inc(qkv_in_psum, 1)
            pe.wait_ge(w_loaded["wlkvT"], 16)
            for c in range(CL):
                last = pe.matmul(bank[7][:], latT[:, c], wlkvT[:, c], start=(c == 0), stop=(c == CL - 1))
            last.then_inc(qkv_in_psum, 1)

            def scores(j):
                for c in range(2):
                    for k, (a, b) in enumerate(((kT_hi, q_hi), (kT_hi, q_lo), (kT_lo, q_hi))):
                        last = pe.matmul(S_BANK[j][:, c * 2 * P:(c + 1) * 2 * P], a[:, j, c], b[:, c],
                                         start=(k == 0), stop=(k == 2))
                return last

            def step(s, r):
                if 0 <= r - 1 < NP:
                    i = s - 1
                    pe.wait_ge(xT_split, i + 1)
                    wait_count(pe, k_in_sbuf, i)
                    for j in range(2):
                        products = ((xT[:, j, 0], wk_hi[:, 0]), (xT[:, j, 0], wk_lo[:, 0]), (xT_lo[:, j], wk_hi[:, 0]),
                                    (xT[:, j, 1], wk_hi[:, 1]), (xT[:, j, 1], wk_lo[:, 1]))
                        for n, (a, b) in enumerate(products):
                            last = pe.matmul(K_BANK[:, j * DL:(j + 1) * DL], a, b, start=(n == 0), stop=(n == len(products) - 1))
                    last.then_inc(k_in_psum, 1)
                if 0 <= r < NP:
                    pe.wait_ge(x_split, s + 1)
                    wait_count(pe, xT_split, s)
                    for j in range(2):
                        turn(XT_BANK[:, 2 * j * P:(2 * j + 1) * P], xh[:, r % 2, j, 0:P])
                        last = turn(XT_BANK[:, (2 * j + 1) * P:(2 * j + 2) * P], x_hl[:, r % RING, j, B_HL].bitcast(F32))
                    last.then_inc(xT_in_psum, 1)
                if 0 <= r - 2 < NP:
                    i = s - 2
                    pe.wait_ge(kn_ready, i + 1)
                    wait_count(pe, kT_split, i)
                    for j in range(2):
                        for c in range(2):
                            last = turn(KT_BANK[:, (2 * j + c) * P:(2 * j + c + 1) * P], kn[:, j, c])
                    last.then_inc(kT_in_psum, 1)
                if 0 <= r - 3 < NP:
                    i = s - 3
                    for j in range(2):
                        first, final = r == 3 and j == 0, r - 3 == NP - 1 and j == 1
                        a_hi, a_lo, b_hl = (x_hl[:, (r - 3) % RING, j, part] for part in (A_HI, A_LO, B_HL))
                        pe.wait_ge(e_hi_ready, 2 * i + j + 1)
                        pe.matmul(U_BANK[0][:], a_hi, e_hi[:, j], start=first, stop=False)
                        pe.matmul(U_BANK[0][:], a_lo, e_hi[:, j], start=False, stop=False)
                        pe.matmul(U_BANK[1][:], b_hl, e_hi[:, j], start=first, stop=False)
                        pe.wait_ge(e_split, 2 * i + j + 1)
                        pe.matmul(U_BANK[1][:], b_hl, e_lo[:, j], start=False, stop=final)
                        pe.matmul(U_BANK[0][:], a_hi, e_lo[:, j], start=False, stop=final).then_inc(probs_used, 1)
                if 0 <= r - 2 < NP:
                    i = s - 2
                    pe.wait_ge(kT_split, i + 1)
                    for j in range(2):
                        wait_count(pe, probs_ready, 2 * i + j - 1)
                        scores(j).then_inc(scores_ready, 1)

            step(0, 0)
            pe.wait_ge(qk_normed, 1)
            pe.wait_ge(prep_done, 1)
            for a in range(2):
                for c in range(2):
                    last = turn(bank[5 + a][:, c * P:(c + 1) * P], qk[:, a, c * P:(c + 1) * P])
                last.then_inc(qkT_in_psum, 1)
            step(1, 1)
            pe.wait_ge(q_split, 1)
            pe.wait_ge(own_kT_split, 1)
            scores(0).then_inc(own_scores, 1)
            pe.wait_ge(own_probs, 1)
            run_steps(pe, step, 2, LOOP_FIRST, LOOP_END, LAST)

            pe.wait_ge(v_own_ready, 2)
            pe.wait_ge(uT_ready, 2)
            for h in range(H):
                o = bank[7][:, h * (DH + 1):(h + 1) * (DH + 1)]
                pe.matmul(o, e_own[:, h * P:(h + 1) * P], v_own[:, h], start=True, stop=False)
                for c in range(2):
                    last = pe.matmul(o, uT[:, c, h * P:(h + 1) * P], wv[:, c, h], start=False, stop=(c == 1))
            last.then_inc(heads_in_psum, 1)
            pe.wait_ge(o_ready, 1)
            for c in range(CL):
                last = turn(bank[2][:, c * P:(c + 1) * P], o_sb[:, c * P:(c + 1) * P])
            last.then_inc(oT_in_psum, 1)
            pe.wait_ge(oT_ready, 1)
            pe.wait_ge(w_loaded["woT"], 16)
            pe.wait_ge(small_loaded, 16 * SMALL)
            pe.matmul(bank[4][:, 0:DL], ones_row[:], bo_row[:], start=True, stop=False)
            for c in range(CL):
                last = pe.matmul(bank[4][:, 0:DL], oT[:, c], woT[:, c], start=False, stop=(c == CL - 1))
            last.then_inc(attn_in_psum, 1)

            for l in range(2):
                pe.wait_ge(xn_ready, l + 1)
                for c in range(CL):
                    last = turn(bank[2][:, c * P:(c + 1) * P], lat[0][:, c * P:(c + 1) * P])
                last.then_inc(xnT_in_psum, 1)
                pe.wait_ge(xnT_ready, l + 1)
                if l == 0:
                    pe.matmul(bank[3][:, 0:E], ones_row[:], bg_row[:], start=True, stop=False)
                for c in range(CL):
                    last = pe.matmul(bank[3][:, 0:E], latT[:, c], wg[l][:, c], start=(l == 1 and c == 0), stop=(c == CL - 1))
                last.then_inc(logits_in_psum, 1)
                pe.wait_ge(experts_loaded[l], 16 * 8)

                def hidden(e):
                    n = l * E + e
                    wait_count(pe, h_ready, n - 1)
                    for c in range(HC):
                        for d in range(CL):
                            last = pe.matmul(bank[6 + n % 2][:, c * P:(c + 1) * P], w1[l][:, e * CL + d, c * P:(c + 1) * P],
                                             latT[:, d], start=(d == 0), stop=(d == CL - 1))
                    last.then_inc(h_in_psum, 1)

                hidden(0)
                pe.wait_ge(wgt_ready, l + 1)
                turn(bank[4][0:E, 0:P], wgt[:]).then_inc(wgtT_in_psum, 1)
                pe.wait_ge(wgtT_ready, l + 1)
                pe.matmul(bank[5][:, 0:DL], wgtT[:], b2[l][:], start=True, stop=True).then_inc(b2_in_psum, 1)
                for e in range(E):
                    n = l * E + e
                    if e + 1 < E:
                        hidden(e + 1)
                    pe.wait_ge(h_ready, n + 1)
                    wait_count(pe, y_added, n - 1)
                    for c in range(HC):
                        last = pe.matmul(bank[n % 2][:, 0:DL], hT[:, n % 2, c], w2[l][:, e * HC + c], start=(c == 0), stop=(c == HC - 1))
                    last.then_inc(y_in_psum, 1)


_OUT = ("out", (1, 128, 256))


def kernel(**inputs):
    import numpy as np
    import concourse.bacc as bacc
    from concourse.bass_utils import run_bass_kernel_spmd

    nc = bacc.Bacc("TRN2", target_bir_lowering=False, num_devices=1)
    layout = {name: np.asarray(value) for name, value in inputs.items()}
    w = {name: layout.pop(f"L0_xattn_{name}") for name in
         ("Wq", "Wkv", "Wlkv", "Wo", "ln_x_g", "ln_x_b", "ln_l_g", "ln_l_b", "qn_g", "kn_g")}
    layout["wqT"], layout["wlkvT"], layout["woT"] = w["Wq"].T, w["Wlkv"].T, w["Wo"].T

    def chunks(a):
        return np.stack([a[:P], np.concatenate([a[P:], a[P:]])])

    layout["wkvT"] = chunks(w["Wkv"].T)
    columns = [w["ln_l_g"].reshape(-1, P).T, w["ln_l_b"].reshape(-1, P).T, chunks(w["ln_x_g"]).T, chunks(w["ln_x_b"]).T,
               np.tile(w["qn_g"], 2)[:, None], np.tile(w["kn_g"], 2)[:, None]]
    for n in ("attn", "ffn"):
        gate = layout.pop(f"L0_{n}_Wg")
        columns.append(gate.reshape(-1, P, gate.shape[1]).transpose(1, 0, 2).reshape(P, -1))
    for n in ("attn", "ffn"):
        columns.append(layout.pop(f"L0_{n}_b1").reshape(-1, P).T)
    layout["columns"] = np.concatenate(columns, axis=1)
    arrays, tensors = {}, {}
    for name, value in layout.items():
        a = np.ascontiguousarray(value)
        arrays[f"in_{name}"] = a
        tensors[name] = nc.dram_tensor(f"in_{name}", a.shape, mybir.dt.from_np(a.dtype), kind="ExternalInput").ap()
    out = nc.dram_tensor(_OUT[0], _OUT[1], F32, kind="ExternalOutput").ap()
    perceiver_block(nc, tensors, out)
    return run_bass_kernel_spmd(nc, [arrays], core_ids=[0]).results[0][_OUT[0]]
```

```python
from contextlib import ExitStack

import concourse.bass as bass
from concourse import mybir

P = 128
ALU = mybir.AluOpType
ACT = mybir.ActivationFunctionType
F32 = mybir.dt.float32
F32R = mybir.dt.float32r
U8 = mybir.dt.uint8
AX_X = mybir.AxisListType.X
ABSMAX = bass.bass_isa.ReduceOp.absmax

LN_EPS = 1e-5
RMS_FLOOR = 1e-8
MASKED = 1e30
SAFE = 60.0
RING = 4
WARM_UP = 24
KEEP_UP = 8, 6, 4, 14, 22
QUARTERS = 2


def wait_count(eng, sem, value):
    if isinstance(value, int) and value <= 0:
        return
    eng.wait_ge(sem, value)


def run_steps(eng, step, first, loop_first, loop_end, last):
    for s in range(first, loop_first):
        step(s, s)
    with eng.Fori(0, (loop_end - loop_first) // RING) as turn:
        for u in range(RING):
            step(turn * RING + (loop_first + u), loop_first + u)
    for s in range(loop_end, last + 1):
        step(s, s)


def perceiver_block(nc, t, out):
    NCTX, DC = t["ctx_768"].shape[1:]
    _, NL, DL = t["x"].shape
    DH = 64
    H = DL // DH
    E, _, HID = t["L0_attn_W1"].shape
    NT = NCTX // P
    NP = NT // 2
    CX = DC - P
    ONE = DC - 1
    CL = DL // P
    HC = HID // P
    SCALE = float(DH) ** -0.5
    assert NL == P and DL == 2 * P and NT == 2 * NP and H * NL == 512 and CX == P // 2

    FIRST, LAST = -2, NP - 1 + 3
    LOOP_FIRST = 4
    LOOP_END = LOOP_FIRST + (NP - 2 - LOOP_FIRST) // RING * RING

    with ExitStack() as ctx:
        def sb(name, shape, dt=F32):
            return ctx.enter_context(nc.sbuf_tensor(name, shape, dt))

        def sem(name):
            return ctx.enter_context(nc.semaphore(name))

        bank = [ctx.enter_context(nc.psum_tensor(f"bank{i}", [P, 512], F32)) for i in range(8)]

        w1 = [sb(f"w1_{l}", [P, E * CL, HID]) for l in range(2)]
        w2 = [sb(f"w2_{l}", [P, E * HC, DL]) for l in range(2)]
        prep_area = w2[1][:].rearrange("p a n -> p (a n)")
        prep_used = [0]

        def prep(a, n):
            at = prep_used[0]
            prep_used[0] = at + a * n
            assert prep_used[0] <= E * HC * DL
            return prep_area[:, at:at + a * n].rearrange("p (a n) -> p a n", a=a)

        ident = sb("ident", [P, P])
        ones_row = sb("ones_row", [1, P])
        minus_half = sb("minus_half", [P, 16])
        rank = sb("rank", [P, E])
        cols = sb("cols", [P, t["columns"].shape[1]])
        at = iter(range(cols.shape[1]))

        def column(n=1):
            first = next(at)
            for _ in range(n - 1):
                next(at)
            return cols[:, first:first + n]

        ln_l_g, ln_l_b = column(CL), column(CL)
        ln_x_g, ln_x_b = column(2), column(2)
        qn_g, kn_g = column(), column()
        wg = [column(CL * E).rearrange("p (c e) -> p c e", c=CL) for _ in range(2)]
        b1T = [column(E * HC) for _ in range(2)]
        bo_row = sb("bo_row", [1, DL])
        bg_row = sb("bg_row", [1, E])
        mask_u8 = sb("mask_u8", [P, NT], U8)
        b2 = [sb(f"b2_{l}", [E, DL]) for l in range(2)]

        x_nat = sb("x_nat", [P, DL])
        woT = sb("woT", [P, CL, DL])
        wqT = prep(CL, DL)
        wlkvT = prep(CL, 2 * DL)
        wkvT = prep(2, 2 * DL)
        wk = prep(2, DL)
        last_row = prep(1, P)[0:CX, 0]
        g_last = prep(1, P)[0:CX, 0]
        b_one = prep(2, P)
        one_col = sb("one_col", [P, 1])
        g_col = sb("g_col", [P, 2])
        b_neg = sb("b_neg", [P, 2])
        wk_hi = sb("wk_hi", [P, 2, DL], F32R)
        wk_lo = sb("wk_lo", [P, 2, DL], F32R)
        wv = sb("wv", [P, 2, H, DH + 1])

        lat = [sb(f"lat{n}", [P, DL]) for n in range(2)]
        stats = sb("stats", [P, 6])
        mean_var = sb("mean_var", [P, 2])
        pow_in = sb("pow_in", [P, 2 * H])
        pow_out = sb("pow_out", [P, 2 * H])
        latT = sb("latT", [P, CL, P])
        qk = prep(2, DL)
        qk_sq = prep(2, DL)
        v_own = sb("v_own", [P, H, DH + 1])
        q_gain = sb("q_gain", [P, 2])
        amax = sb("amax", [P, 1])
        shift = sb("shift", [P, 2])
        mask_f = sb("mask_f", [P, NT])
        bias = sb("bias", [P, NT])
        q_bd = prep(2, 2 * P)
        q_hi = sb("q_hi", [P, 2, 2 * P], F32R)
        q_lo = sb("q_lo", [P, 2, 2 * P], F32R)
        e_own = sb("e_own", [P, 512])

        x_in = sb("x_in", [P, RING, 2, DC])
        xh = sb("xh", [P, 2, 2, ONE])
        x_hl = sb("x_hl", [P, RING, 2, 2 * DC], F32R)
        A_HI, B_HL, A_LO = slice(0, P), slice(P, P + 2 * CX), slice(DC + CX, 2 * DC)
        x_stats = sb("x_stats", [P, 2, 6])
        x_mv = sb("x_mv", [P, RING, 2, 2])
        x_var = sb("x_var", [P, 2, 2])
        x_rstd = sb("x_rstd", [P, 2, 2])
        k_ms = sb("k_ms", [P, 2 * H])
        k_rs = sb("k_rs", [P, 2 * H])
        xT = sb("xT", [P, 2, 2, P], F32R)
        xT_lo = sb("xT_lo", [P, 2, P], F32R)
        k_sb = sb("k_sb", [P, 2, 2 * DL])
        k_sq = sb("k_sq", [P, 2 * DL])
        k_ss = sb("k_ss", [P, 2 * H])
        kn = sb("kn", [P, 2, 2, P])
        kT_hi = sb("kT_hi", [P, 2, 2, P], F32R)
        kT_lo = sb("kT_lo", [P, 2, 2, P], F32R)
        e_f32 = sb("e_f32", [P, 2, 512])
        e_hi = sb("e_hi", [P, 2, 512], F32R)
        e_lo = sb("e_lo", [P, 2, 512], F32R)

        own_hi, own_lo = (a[:, 1, 0:2 * P].rearrange("p (c n) -> p c n", c=2) for a in (e_hi, e_lo))

        uT = k_sb
        den_r = sb("den_r", [P, H])
        o_sb = sb("o_sb", [P, DL])
        oT = sb("oT", [P, CL, P])
        x_cur = [sb(f"x_cur{l}", [P, DL]) for l in range(3)]
        g_max = sb("g_max", [P, 4])
        g_e = sb("g_e", [P, E])
        g_p = sb("g_p", [P, 8, E])
        wgt = sb("wgt", [P, E])
        wgtT = sb("wgtT", [E, P])
        hT = e_f32[:].rearrange("p a (c n) -> p a c n", c=HC)

        spare = x_hl[:].rearrange("p r j n -> p (r j n)")
        W2 = HC * DL
        w2_hi = [spare[:, k * W2:(k + 1) * W2].rearrange("p (c n) -> p c n", c=HC) for k in range(2)]
        w2_lo = [a.rearrange("p (c n) -> p c n", c=HC) for a in
                 (spare[:, 2 * W2:3 * W2], e_lo[:].rearrange("p a n -> p (a n)"))]
        h_hi = [e_hi[:, k].rearrange("p (c n) -> p c n", c=HC) for k in range(2)]
        h_lo = [a[:].rearrange("p j c n -> p (j c) n") for a in (kT_hi, kT_lo)]

        U_BANK = [bank[0], bank[1]]
        XT_BANK, K_BANK, KT_BANK = bank[2], bank[3], bank[4]
        S_BANK = [bank[5], bank[6]]

        consts_ready = sem("consts_ready")
        zeros_ready = sem("zeros_ready")
        small_loaded = sem("small_loaded")
        x_nat_loaded = sem("x_nat_loaded")
        w_loaded = {n: sem(f"{n}_loaded") for n in ("wqT", "wkvT", "wlkvT", "woT")}
        cols_loaded = sem("cols_loaded")
        experts_loaded = [sem(f"experts_loaded{l}") for l in range(2)]
        last_gain_ready = sem("last_gain_ready")
        taken_off_in_psum = sem("taken_off_in_psum")
        dve_step = sem("dve_step")
        var_ready = sem("var_ready")
        rstd_ready = sem("rstd_ready")
        lat_ready = sem("lat_ready")
        latT_in_psum = sem("latT_in_psum")
        latT_ready = sem("latT_ready")
        qkv_in_psum = sem("qkv_in_psum")
        qk_ready = sem("qk_ready")
        v_own_ready = sem("v_own_ready")
        qk_normed = sem("qk_normed")
        qkT_in_psum = sem("qkT_in_psum")
        gain_ready = sem("gain_ready")
        amax_ready = sem("amax_ready")
        bias_ready = sem("bias_ready")
        q_split = sem("q_split")
        own_kT_hi = sem("own_kT_hi")
        own_kT_split = sem("own_kT_split")
        own_scores = sem("own_scores")
        own_probs = sem("own_probs")
        prep_done = sem("prep_done")

        x_loaded = [sem(f"x_loaded{k}") for k in range(RING)]
        x_hi_ready = sem("x_hi_ready")
        x_split = sem("x_split")
        x_stats_ready = sem("x_stats_ready")
        x_mv_ready = sem("x_mv_ready")
        k_summed = sem("k_summed")
        k_ms_ready = sem("k_ms_ready")
        k_rs_ready = sem("k_rs_ready")
        x_var_ready = sem("x_var_ready")
        x_rstd_ready = sem("x_rstd_ready")
        xh_ready = sem("xh_ready")
        xT_in_psum = sem("xT_in_psum")
        xT_ready = sem("xT_ready")
        xT_split = sem("xT_split")
        k_in_psum = sem("k_in_psum")
        k_in_sbuf = sem("k_in_sbuf")
        k_squared = sem("k_squared")
        kn_ready = sem("kn_ready")
        kT_in_psum = sem("kT_in_psum")
        kT_hi_ready = sem("kT_hi_ready")
        kT_split = sem("kT_split")
        scores_ready = sem("scores_ready")
        probs_ready = sem("probs_ready")
        e_hi_ready = sem("e_hi_ready")
        e_split = sem("e_split")
        probs_used = sem("probs_used")

        uT_ready = sem("uT_ready")
        heads_in_psum = sem("heads_in_psum")
        o_ready = sem("o_ready")
        oT_in_psum = sem("oT_in_psum")
        oT_ready = sem("oT_ready")
        attn_in_psum = sem("attn_in_psum")
        xn_ready = sem("xn_ready")
        xnT_in_psum = sem("xnT_in_psum")
        xnT_ready = sem("xnT_ready")
        logits_in_psum = sem("logits_in_psum")
        logits_max = sem("logits_max")
        gate_exp = sem("gate_exp")
        wgt_ready = sem("wgt_ready")
        wgtT_in_psum = sem("wgtT_in_psum")
        wgtT_ready = sem("wgtT_ready")
        b2_in_psum = sem("b2_in_psum")
        h_in_psum = sem("h_in_psum")
        h_ready = sem("h_ready")
        h_hi_ready = sem("h_hi_ready")
        h_split = sem("h_split")
        w2_hi_ready = sem("w2_hi_ready")
        w2_split = sem("w2_split")
        y_in_psum = sem("y_in_psum")
        y_added = sem("y_added")
        out_ready = sem("out_ready")
        out_stored = sem("out_stored")

        ctx_rows = t["ctx_768"][0].rearrange("(p a j) d -> a p j d", p=P, j=2)
        SMALL = 5

        block = ctx.enter_context(nc.Block())

        @block.sync
        def _(sp):
            sp.dma_start(x_nat[:], t["x"][0]).then_inc(x_nat_loaded, 16)
            sp.dma_start(wkvT[:], t["wkvT"].rearrange("c p n -> p c n")).then_inc(w_loaded["wkvT"], 16)
            sp.dma_start(wlkvT[:], t["wlkvT"].rearrange("(c p) n -> p c n", p=P)).then_inc(w_loaded["wlkvT"], 16)

            def load(i, r):
                wait_count(sp, xh_ready, i - RING + 1)
                sp.dma_start(x_in[:, r % RING], ctx_rows[bass.ds(i, 1)].rearrange("a p j d -> (a p) j d")
                             if not isinstance(i, int) else ctx_rows[i]).then_inc(x_loaded[r % RING], 16)

            for i in range(RING):
                load(i, i)
            for n, (l, src, dst) in enumerate(((0, t["L0_attn_W1"], w1[0]), (0, t["L0_attn_W2"], w2[0]),
                                               (1, t["L0_ffn_W1"], w1[1]), (1, t["L0_ffn_W2"], w2[1]))):
                rows = src.rearrange("e k n -> (e k) n").rearrange("(a p) n -> p a n", p=P)
                quarter = rows.shape[1] // 4
                if dst is w2[1]:
                    sp.wait_ge(own_probs, 1)
                with sp.Fori(0, 4 // QUARTERS) as turn:
                    for u in range(RING):
                        load((turn + (1 + n * (4 // QUARTERS))) * RING + u, u)
                        if u % (RING // QUARTERS) == 0:
                            part = bass.ds((turn * QUARTERS + u // (RING // QUARTERS)) * quarter, quarter)
                            sp.dma_start(dst[:, part], rows[:, part]).then_inc(experts_loaded[l], 16)
            done = RING * (1 + 16 // QUARTERS)
            run_steps(sp, load, done, done, done + (NP - done) // RING * RING, NP - 1)
            sp.wait_ge(out_ready, 1)
            sp.dma_start(out[0], x_cur[2][:]).then_inc(out_stored, 16)
            sp.wait_ge(out_stored, 16)

        @block.gpsimd
        def _(gp):
            gp.memset(ident[:], 0.0).then_inc(zeros_ready, 1)
            gp.memset(last_row, 0.0).then_inc(zeros_ready, 1)
            gp.memset(minus_half[:], -0.5).then_inc(consts_ready, 1)
            gp.memset(ones_row[:], 1.0).then_inc(consts_ready, 1)
            gp.wait_ge(zeros_ready, 2)
            gp.affine_select(out=ident[:], in_=ident[:], compare_op=ALU.not_equal, fill=1.0, base=0,
                             pattern=[[-1, P]], channel_multiplier=1).then_inc(consts_ready, 1)
            gp.affine_select(out=last_row, in_=last_row, compare_op=ALU.not_equal, fill=1.0, base=1 - CX,
                             pattern=[[0, P]], channel_multiplier=1).then_inc(consts_ready, 1)
            gp.iota(rank[:], [[-1, E]], base=E, channel_multiplier=0,
                    allow_small_or_imprecise_dtypes=True).then_inc(consts_ready, 1)

            def power(n, cols):
                gp.wait_ge(var_ready, n)
                gp.tensor_tensor(pow_out[:, 0:cols], pow_in[:, 0:cols], minus_half[:, 0:cols], ALU.pow).then_inc(rstd_ready, 1)

            gp.wait_ge(consts_ready, 5)
            power(1, 1)
            power(2, 1)
            gp.wait_ge(gain_ready, 1)
            gp.partition_all_reduce(amax[:], q_gain[:, 0:1], P, ABSMAX).then_inc(amax_ready, 1)

            def step(s, r):
                if 0 <= r + 1 < NP:
                    gp.wait_ge(x_var_ready, s + 1 + 1)
                    gp.tensor_tensor(x_rstd[:, (r + 1) % 2], x_var[:, (r + 1) % 2], minus_half[:, 0:2], ALU.pow).then_inc(x_rstd_ready, 1)
                if r == 0:
                    power(3, 2 * H)
                if 0 <= r - 1 < NP:
                    i = s - 1
                    gp.wait_ge(k_ms_ready, i + 1)
                    wait_count(gp, kn_ready, i)
                    gp.tensor_tensor(k_rs[:], k_ms[:], minus_half[:, 0:2 * H], ALU.pow).then_inc(k_rs_ready, 1)
                    gp.wait_ge(k_in_sbuf, i + 1)
                    gp.wait_ge(k_rs_ready, i + 1)
                    wait_count(gp, kT_in_psum, i)
                    gp.tensor_tensor(kn[:].rearrange("p j c (g d) -> p (j c g) d", d=DH),
                                     k_sb[:, (r - 1) % 2].rearrange("p (g d) -> p g d", d=DH),
                                     k_rs[:].unsqueeze(2).broadcast_to([P, 2 * H, DH]),
                                     ALU.mult).then_inc(kn_ready, 1)
                if 0 <= r + 1 < NP:
                    i = s + 1
                    gp.wait_ge(x_hi_ready, i + 1)
                    both = x_hl[:, (r + 1) % RING]
                    gp.tensor_tensor(both[:, :, A_LO], xh[:, (r + 1) % 2, :, 0:P], both[:, :, A_HI].bitcast(F32), ALU.subtract)
                    gp.tensor_tensor(both[:, :, DC:DC + CX - 1], xh[:, (r + 1) % 2, :, P:ONE],
                                     both[:, :, P:ONE].bitcast(F32), ALU.subtract).then_inc(x_split, 1)

            step(-2, -2)
            step(-1, -1)
            run_steps(gp, step, 0, LOOP_FIRST, LOOP_END, LAST)

            def split_w2(first, end):
                for n in range(first, end):
                    gp.wait_ge(w2_hi_ready, n + 1)
                    wait_count(gp, y_in_psum, n - 1)
                    gp.tensor_tensor(w2_lo[n % 2], w2[n // E][:, (n % E) * HC:(n % E + 1) * HC],
                                     w2_hi[n % 2].bitcast(F32), ALU.subtract).then_inc(w2_split, 1)

            split_w2(0, 2)
            power(4, 1)
            split_w2(2, E + 1)
            power(5, 1)
            split_w2(E + 1, 2 * E)

        @block.scalar
        def _(act):
            act.dma_start(cols[:], t["columns"]).then_inc(cols_loaded, 16)
            act.dma_start(wqT[:], t["wqT"].rearrange("(c p) n -> p c n", p=P)).then_inc(w_loaded["wqT"], 16)
            act.dma_start(mask_u8[:], t["mask_BxS2_bk0"][0].rearrange("(p a) -> p a", p=P)).then_inc(small_loaded, 16)
            act.dma_start(bo_row[:], t["L0_xattn_bo"].rearrange("(a n) -> a n", a=1)).then_inc(small_loaded, 16)
            act.dma_start(bg_row[:], t["L0_attn_bg"].rearrange("(a n) -> a n", a=1)).then_inc(small_loaded, 16)
            for l, n in enumerate(("attn", "ffn")):
                act.dma_start(b2[l][:], t[f"L0_{n}_b2"]).then_inc(small_loaded, 16)
            act.dma_start(woT[:], t["woT"].rearrange("(c p) n -> p c n", p=P)).then_inc(w_loaded["woT"], 16)

            def split_probs(i, j):
                act.wait_ge(probs_ready, 2 * i + j + 1)
                wait_count(act, probs_used, 2 * (i - 1) + j + 1)
                act.activation(e_hi[:, j], e_f32[:, j], ACT.Copy).then_inc(e_hi_ready, 1)

            def exponentials(i, j):
                act.wait_ge(scores_ready, 2 * i + j + 1)
                wait_count(act, e_split, 2 * (i - 1) + j + 1)
                tile = 2 * i + j
                b = bias[:, tile:tile + 1] if isinstance(i, int) else bias[:, bass.ds(tile, 1)]
                act.activation(e_f32[:, j], S_BANK[j][:], ACT.Exp, bias=b).then_inc(probs_ready, 1)

            def step(s, r):
                if 0 <= r - 1 < NP:
                    i = s - 1
                    act.wait_ge(k_in_psum, i + 1)
                    wait_count(act, k_summed, i)
                    act.activation(k_sq[:], K_BANK[:], ACT.Square).then_inc(k_squared, 1)
                if 0 <= r - 3 < NP:
                    split_probs(s - 3, 1)
                if 0 <= r - 2 < NP:
                    i = s - 2
                    act.wait_ge(kT_in_psum, i + 1)
                    wait_count(act, scores_ready, 2 * i)
                    act.activation(kT_hi[:].rearrange("p j c n -> p (j c n)"), KT_BANK[:], ACT.Copy).then_inc(kT_hi_ready, 1)
                if 0 <= r - 1 < NP:
                    i = s - 1
                    wait_count(act, kn_ready, i - 1)
                    act.activation(k_sb[:, (r - 1) % 2], K_BANK[:], ACT.Copy).then_inc(k_in_sbuf, 1)
                if 0 <= r < NP:
                    act.wait_ge(xT_in_psum, s + 1)
                    wait_count(act, k_in_psum, s)
                    act.activation(xT[:].rearrange("p j c n -> p (j c n)"), XT_BANK[:], ACT.Copy).then_inc(xT_ready, 1)
                if 0 <= r + 1 < NP:
                    i = s + 1
                    act.wait_ge(xh_ready, i + 1)
                    wait_count(act, probs_used, 2 * (i - RING) + 2)
                    act.activation(x_hl[:, (r + 1) % RING, :, 0:ONE], xh[:, (r + 1) % 2], ACT.Copy).then_inc(x_hi_ready, 1)
                if 0 <= r - 2 < NP:
                    exponentials(s - 2, 0)
                    split_probs(s - 2, 0)
                    exponentials(s - 2, 1)

            step(-2, -2)
            step(-1, -1)
            act.wait_ge(qkv_in_psum, 1)
            act.activation(qk[:, 0], bank[1][:, 0:DL], ACT.Copy).then_inc(qk_ready, 1)
            act.wait_ge(qkv_in_psum, 2)
            act.activation(qk[:, 1], bank[7][:, 0:DL], ACT.Copy).then_inc(qk_ready, 1)
            act.activation(v_own[:, :, 0:DH], bank[7][:, DL:2 * DL].rearrange("p (h d) -> p h d", d=DH),
                           ACT.Copy).then_inc(v_own_ready, 1)
            step(0, 0)
            step(1, 1)
            act.wait_ge(qkT_in_psum, 2)
            act.activation(own_hi, bank[6][:, 0:2 * P].rearrange("p (c n) -> p c n", c=2), ACT.Copy).then_inc(own_kT_hi, 1)
            act.wait_ge(bias_ready, 1)
            step(2, 2)
            act.wait_ge(own_scores, 1)
            act.activation(e_own[:], bank[7][:], ACT.Exp, bias=shift[:, 1:2]).then_inc(own_probs, 1)
            run_steps(act, step, 3, LOOP_FIRST, LOOP_END, LAST)

            act.wait_ge(probs_used, 2 * NP)
            act.activation(uT[:, 0], U_BANK[0][:], ACT.Copy).then_inc(uT_ready, 1)
            act.wait_ge(experts_loaded[0], 16 * 8)

            def w2_high(n):
                wait_count(act, y_in_psum, n - 1)
                act.activation(w2_hi[n % 2], w2[n // E][:, (n % E) * HC:(n % E + 1) * HC], ACT.Copy).then_inc(w2_hi_ready, 1)

            w2_high(0)
            w2_high(1)
            act.wait_ge(oT_in_psum, 1)
            act.activation(oT[:].rearrange("p c n -> p (c n)"), bank[2][:, 0:DL], ACT.Copy).then_inc(oT_ready, 1)
            for l in range(2):
                act.wait_ge(xnT_in_psum, l + 1)
                act.activation(latT[:].rearrange("p c n -> p (c n)"), bank[2][:, 0:DL], ACT.Copy).then_inc(xnT_ready, 1)
                act.wait_ge(logits_max, l + 1)
                act.activation(g_e[:], bank[3][:, 0:E], ACT.Exp, bias=g_max[:, 0:1]).then_inc(gate_exp, 1)
                for e in range(E):
                    n = l * E + e
                    if e >= 2:
                        w2_high(n)
                    act.wait_ge(h_in_psum, n + 1)
                    wait_count(act, h_split, n - 1)
                    for c in range(HC):
                        last = act.activation(hT[:, n % 2, c], bank[6 + n % 2][:, c * P:(c + 1) * P], ACT.Relu,
                                              bias=b1T[l][:, e * HC + c:e * HC + c + 1])
                    last.then_inc(h_ready, 1)
                    wait_count(act, y_in_psum, n - 1)
                    act.wait_ge(h_ready, n + 1)
                    act.activation(h_hi[n % 2], hT[:, n % 2], ACT.Copy).then_inc(h_hi_ready, 1)
                if l == 0:
                    act.wait_ge(experts_loaded[1], 16 * 8)
                    w2_high(E)
                    w2_high(E + 1)

        @block.vector
        def _(dve):
            chain = [0]

            def link(ins):
                chain[0] += 1
                ins.then_inc(dve_step, 1)
                dve.wait_ge(dve_step, chain[0])

            def norm(n, dst, src):
                variance(src)
                return normalise(n, dst, src)

            def variance(src):
                link(dve.bn_stats(stats[:], src))
                link(dve.bn_aggr(mean_var[:], stats[:]))
                dve.tensor_scalar(pow_in[:, 0:1], mean_var[:, 1:2], LN_EPS, None, ALU.add).then_inc(var_ready, 1)

            def normalise(n, dst, src):
                dve.wait_ge(rstd_ready, n)
                return dve.tensor_scalar(dst, src, mean_var[:, 0:1], pow_out[:, 0:1], ALU.subtract, ALU.mult)

            def slot_loads(i, r):
                if isinstance(i, int):
                    return 16 * (i // RING + 1)
                return (i - r % RING) * (16 // RING) + 16

            def split_probs(s, j):
                n = 2 * (s - 3) + j + 1
                dve.wait_ge(e_hi_ready, n)
                wait_count(dve, probs_used, n - 2)
                dve.tensor_tensor(e_lo[:, j], e_f32[:, j], e_hi[:, j].bitcast(F32), ALU.subtract).then_inc(e_split, 1)

            def aggregates(i, r):
                for j in range(2):
                    last = dve.bn_aggr(x_mv[:, r % RING, j], x_stats[:, j])
                last.then_inc(x_mv_ready, 1)
                dve.wait_ge(x_mv_ready, i + 1)
                dve.tensor_scalar(x_var[:, r % 2], x_mv[:, r % RING, :, 1], LN_EPS, None, ALU.add).then_inc(x_var_ready, 1)

            def step(s, r):
                if 3 <= r < NP - 1:
                    dve.wait_ge(x_stats_ready, s + 2)
                if 0 <= r - 3 < NP:
                    split_probs(s, 0)
                if 3 <= r < NP - 1:
                    aggregates(s + 1, r + 1)
                if 0 <= r - 1 < NP:
                    i = s - 1
                    dve.wait_ge(k_squared, i + 1)
                    dve.tensor_reduce(k_ss[:], k_sq[:].rearrange("p (g d) -> p g d", d=DH), AX_X, ALU.add).then_inc(k_summed, 1)
                if 0 <= r - 3 < NP:
                    split_probs(s, 1)
                if 0 <= r - 1 < NP:
                    i = s - 1
                    dve.wait_ge(k_summed, i + 1)
                    wait_count(dve, k_rs_ready, i)
                    dve.tensor_scalar(k_ms[:], k_ss[:], 1.0 / DH, RMS_FLOOR ** 2, ALU.mult, ALU.max).then_inc(k_ms_ready, 1)
                if 0 <= r - 2 < NP:
                    dve.wait_ge(kT_hi_ready, s - 2 + 1)
                    dve.tensor_tensor(kT_lo[:].rearrange("p j c n -> p (j c n)"), KT_BANK[:],
                                      kT_hi[:].rearrange("p j c n -> p (j c n)").bitcast(F32), ALU.subtract).then_inc(kT_split, 1)
                if 0 <= r + 1 < NP:
                    i, slot = s + 1, (r + 1) % RING
                    dve.wait_ge(x_rstd_ready, i + 1)
                    wait_count(dve, x_split, i - 1)
                    wait_count(dve, xT_in_psum, i - 1)
                    for j in range(2):
                        last = dve.tensor_scalar(xh[:, (r + 1) % 2, j], x_in[:, slot, j, 0:ONE], x_mv[:, slot, j, 0:1],
                                                 x_rstd[:, (r + 1) % 2, j:j + 1], ALU.subtract, ALU.mult)
                    last.then_inc(xh_ready, 1)
                if 0 <= r < NP:
                    dve.wait_ge(xT_ready, s + 1)
                    dve.tensor_tensor(xT_lo[:], XT_BANK[:].rearrange("p (j c n) -> p j c n", j=2, c=2)[:, :, 0],
                                      xT[:, :, 0].bitcast(F32), ALU.subtract).then_inc(xT_split, 1)
                if r + 2 < NP:
                    slot = (r + 2) % RING
                    dve.wait_ge(x_loaded[slot], slot_loads(s + 2, r + 2))
                    for j in range(2):
                        last = dve.bn_stats(x_stats[:, j], x_in[:, slot, j])
                    last.then_inc(x_stats_ready, 1)
                if r < 2:
                    dve.wait_ge(x_stats_ready, s + 3)
                    aggregates(s + 2, r + 2)

            dve.memset(q_bd[:], 0.0)
            dve.memset(b_one[:], 0.0)
            dve.memset(v_own[:, :, DH:DH + 1], 1.0).then_inc(v_own_ready, 1)
            dve.memset(x_hl[:, :, :, DC + CX - 1:DC + CX].bitcast(F32), 0.0)
            dve.memset(wv[:, 0, :, DH:DH + 1], 0.0)
            link(dve.memset(x_hl[:, :, :, ONE:DC].bitcast(F32), 1.0))
            dve.wait_ge(x_nat_loaded, 16)
            variance(x_nat[:])
            dve.wait_ge(consts_ready, 5)
            link(dve.tensor_tensor(one_col[:], ident[:, CX - 1:CX], ident[:, P - 1:P], ALU.add))
            dve.wait_ge(cols_loaded, 16)
            link(dve.tensor_scalar(b_neg[:], ln_x_b, -1.0, None, ALU.mult))
            link(normalise(1, lat[0][:], x_nat[:]))
            variance(lat[0][:])
            dve.tensor_scalar(g_last, last_row, ln_x_g[0:CX, 1:2], None, ALU.mult)
            dve.tensor_scalar(b_one[0:CX, 1], last_row, ln_x_g[0:CX, 1:2], None, ALU.mult)
            link(dve.tensor_copy(b_one[:, 0, CX - 1::CX], b_neg[:, 0:1].broadcast_to([P, 2])))
            dve.tensor_copy(b_one[0:CX, 1, CX - 1::CX], b_neg[0:CX, 1:2].broadcast_to([CX, 2])).then_inc(last_gain_ready, 1)
            normalise(2, lat[1][:], lat[0][:]).then_inc(lat_ready, 1)
            link(dve.tensor_tensor(q_gain[:, 0:1], qn_g, kn_g, ALU.mult))
            dve.tensor_scalar(q_gain[:, 1:2], q_gain[:, 0:1], SCALE, None, ALU.mult).then_inc(gain_ready, 1)
            step(-2, -2)
            dve.wait_ge(latT_in_psum, 1)
            for c in range(CL):
                last = dve.tensor_scalar(latT[:, c], bank[0][:, c * P:(c + 1) * P], ln_l_g[:, c:c + 1],
                                         ln_l_b[:, c:c + 1], ALU.mult, ALU.add)
            last.then_inc(latT_ready, 1)
            dve.tensor_copy(g_col[:, 0:1], ln_x_g[:, 0:1])
            dve.tensor_tensor(g_col[:, 1:2], one_col[:], ln_x_g[:, 1:2], ALU.mult)
            link(dve.tensor_copy(wv[:, 1, :, DH], one_col[:].broadcast_to([P, H])))
            link(dve.tensor_tensor(g_col[:, 1:2], ln_x_g[:, 1:2], g_col[:, 1:2], ALU.subtract))
            step(-1, -1)
            dve.wait_ge(taken_off_in_psum, 1)
            for c in range(2):
                dve.scalar_tensor_tensor(out=wk[:, c], in0=wkvT[:, c, 0:DL], scalar=g_col[:, c:c + 1],
                                         in1=bank[5 + c][:, 0:DL], op0=ALU.mult, op1=ALU.subtract)
                last = dve.scalar_tensor_tensor(out=wv[:, c, :, 0:DH], in0=wkvT[:, c, DL:2 * DL].rearrange("p (h d) -> p h d", d=DH),
                                                scalar=g_col[:, c:c + 1],
                                                in1=bank[5 + c][:, DL:2 * DL].rearrange("p (h d) -> p h d", d=DH),
                                                op0=ALU.mult, op1=ALU.subtract)
            link(last)
            link(dve.tensor_copy(wk_hi[:], wk[:]))
            dve.tensor_tensor(wk_lo[:], wk[:], wk_hi[:].bitcast(F32), ALU.subtract).then_inc(prep_done, 1)
            dve.wait_ge(qk_ready, 2)
            link(dve.tensor_tensor(qk_sq[:], qk[:], qk[:], ALU.mult))
            link(dve.tensor_reduce(pow_in[:], qk_sq[:].rearrange("p a (h d) -> p (a h) d", d=DH), AX_X, ALU.add))
            dve.tensor_scalar(pow_in[:], pow_in[:], 1.0 / DH, RMS_FLOOR ** 2, ALU.mult, ALU.max).then_inc(var_ready, 1)
            step(0, 0)
            dve.wait_ge(amax_ready, 1)
            link(dve.tensor_scalar(shift[:, 0:1], amax[:], -SCALE * DH, SAFE, ALU.mult, ALU.add))
            link(dve.tensor_scalar(shift[:, 1:2], shift[:, 0:1], 0.0, None, ALU.min))
            dve.wait_ge(small_loaded, 16 * SMALL)
            link(dve.tensor_scalar(mask_f[:], mask_u8[:], MASKED, -MASKED, ALU.mult, ALU.add))
            dve.tensor_scalar(bias[:], mask_f[:], shift[:, 1:2], None, ALU.add).then_inc(bias_ready, 1)
            dve.wait_ge(rstd_ready, 3)
            dve.tensor_tensor(qk[:].rearrange("p a (h d) -> p (a h) d", d=DH), qk[:].rearrange("p a (h d) -> p (a h) d", d=DH),
                              pow_out[:].unsqueeze(2).broadcast_to([P, 2 * H, DH]), ALU.mult).then_inc(qk_normed, 1)
            step(1, 1)
            dve.wait_ge(qkT_in_psum, 1)
            for half in range(2):
                rows = slice(half * DH, (half + 1) * DH)
                last = dve.tensor_scalar(q_bd[rows, :, half * P:(half + 1) * P],
                                         bank[5][rows, 0:2 * P].rearrange("p (c n) -> p c n", c=2),
                                         q_gain[rows, 1:2], None, ALU.mult)
            link(last)
            link(dve.tensor_copy(q_hi[:], q_bd[:]))
            dve.tensor_tensor(q_lo[:], q_bd[:], q_hi[:].bitcast(F32), ALU.subtract).then_inc(q_split, 1)
            dve.wait_ge(own_kT_hi, 1)
            dve.tensor_tensor(own_lo, bank[6][:, 0:2 * P].rearrange("p (c n) -> p c n", c=2),
                              own_hi.bitcast(F32), ALU.subtract).then_inc(own_kT_split, 1)

            run_steps(dve, step, 2, LOOP_FIRST, LOOP_END, LAST)

            dve.wait_ge(probs_used, 2 * NP)
            dve.tensor_copy(uT[:, 1], U_BANK[1][:]).then_inc(uT_ready, 1)
            dve.wait_ge(heads_in_psum, 1)
            heads = bank[7][:, 0:H * (DH + 1)].rearrange("p (h d) -> p h d", d=DH + 1)
            link(dve.reciprocal(den_r[:], heads[:, :, DH]))
            dve.tensor_tensor(o_sb[:].rearrange("p (h d) -> p h d", d=DH), heads[:, :, 0:DH],
                              den_r[:].unsqueeze(2).broadcast_to([P, H, DH]), ALU.mult).then_inc(o_ready, 1)
            dve.wait_ge(attn_in_psum, 1)
            link(dve.tensor_tensor(x_cur[0][:], bank[4][:, 0:DL], x_nat[:], ALU.add))

            def split_h(n):
                dve.wait_ge(h_hi_ready, n + 1)
                wait_count(dve, y_in_psum, n - 1)
                dve.tensor_tensor(h_lo[n % 2], hT[:, n % 2], h_hi[n % 2].bitcast(F32), ALU.subtract).then_inc(h_split, 1)

            for l in range(2):
                norm(3 + l + 1, lat[0][:], x_cur[l][:]).then_inc(xn_ready, 1)
                p, cand, first, rest, cand2, second, w_a, w_b = (g_p[:, k] for k in range(8))
                dve.wait_ge(logits_in_psum, l + 1)
                dve.tensor_reduce(g_max[:, 0:1], bank[3][:, 0:E], AX_X, ALU.max, negate=True).then_inc(logits_max, 1)
                dve.wait_ge(gate_exp, l + 1)
                link(dve.tensor_reduce(g_max[:, 1:2], g_e[:], AX_X, ALU.add))
                link(dve.reciprocal(g_max[:, 2:3], g_max[:, 1:2]))
                link(dve.tensor_scalar(p, g_e[:], g_max[:, 2:3], None, ALU.mult))
                link(dve.tensor_reduce(g_max[:, 0:1], p, AX_X, ALU.max))
                link(dve.scalar_tensor_tensor(out=cand, in0=p, scalar=g_max[:, 0:1], in1=rank[:], op0=ALU.is_equal, op1=ALU.mult))
                link(dve.tensor_reduce(g_max[:, 1:2], cand, AX_X, ALU.max))
                link(dve.tensor_scalar(first, cand, g_max[:, 1:2], None, ALU.is_equal))
                if l == 0:
                    dve.tensor_tensor(wgt[:], first, p, ALU.mult).then_inc(wgt_ready, 1)
                else:
                    link(dve.scalar_tensor_tensor(out=rest, in0=first, scalar=-2.0, in1=p, op0=ALU.mult, op1=ALU.add))
                    link(dve.tensor_reduce(g_max[:, 1:2], rest, AX_X, ALU.max))
                    link(dve.scalar_tensor_tensor(out=cand2, in0=rest, scalar=g_max[:, 1:2], in1=rank[:], op0=ALU.is_equal, op1=ALU.mult))
                    link(dve.tensor_reduce(g_max[:, 2:3], cand2, AX_X, ALU.max))
                    link(dve.tensor_scalar(second, cand2, g_max[:, 2:3], None, ALU.is_equal))
                    link(dve.tensor_tensor(w_a, first, second, ALU.add))
                    link(dve.tensor_tensor(w_b, w_a, p, ALU.mult))
                    link(dve.tensor_tensor(g_max[:, 3:4], g_max[:, 0:1], g_max[:, 1:2], ALU.add))
                    link(dve.reciprocal(g_max[:, 2:3], g_max[:, 3:4]))
                    dve.tensor_scalar(wgt[:], w_b, g_max[:, 2:3], None, ALU.mult).then_inc(wgt_ready, 1)
                split_h(l * E)
                dve.wait_ge(wgtT_in_psum, l + 1)
                dve.tensor_copy(wgtT[:], bank[4][0:E, 0:P]).then_inc(wgtT_ready, 1)
                split_h(l * E + 1)
                dve.wait_ge(b2_in_psum, l + 1)
                link(dve.tensor_tensor(x_cur[l + 1][:], bank[5][:, 0:DL], x_cur[l][:], ALU.add))
                for e in range(E):
                    n = l * E + e
                    dve.wait_ge(y_in_psum, n + 1)
                    last = dve.scalar_tensor_tensor(out=x_cur[l + 1][:], in0=bank[n % 2][:, 0:DL], scalar=wgt[:, e:e + 1],
                                                    in1=x_cur[l + 1][:], op0=ALU.mult, op1=ALU.add)
                    last.then_inc(y_added, 1)
                    if e + 2 < E:
                        split_h(n + 2)
                    dve.wait_ge(y_added, n + 1)
            dve.tensor_copy(x_cur[0][0:1, 0:1], x_cur[2][0:1, 0:1]).then_inc(out_ready, 1)

        @block.tensor
        def _(pe):
            def keep_up(n):
                for _ in range(n):
                    turn(bank[3][:, 0:P], ident[:])

            def turn(dst, src):
                return pe.transpose(dst, src, ident[0:src.shape[0], 0:src.shape[0]])

            pe.wait_ge(consts_ready, 5)
            keep_up(WARM_UP)
            pe.wait_ge(lat_ready, 1)
            for c in range(CL):
                last = turn(bank[0][:, c * P:(c + 1) * P], lat[1][:, c * P:(c + 1) * P])
            last.then_inc(latT_in_psum, 1)
            pe.wait_ge(w_loaded["wkvT"], 16)
            pe.wait_ge(last_gain_ready, 1)
            pe.matmul(bank[5][:], g_last, wkvT[0:CX, 1], start=True, stop=True)
            pe.matmul(bank[6][:], b_one[:, 0], wkvT[:, 0], start=True, stop=False)
            pe.matmul(bank[6][:], b_one[0:CX, 1], wkvT[0:CX, 1], start=False, stop=True).then_inc(taken_off_in_psum, 1)
            pe.wait_ge(latT_ready, 1)
            pe.wait_ge(w_loaded["wqT"], 16)
            for c in range(CL):
                last = pe.matmul(bank[1][:, 0:DL], latT[:, c], wqT[:, c], start=(c == 0), stop=(c == CL - 1))
            last.then_inc(qkv_in_psum, 1)
            pe.wait_ge(w_loaded["wlkvT"], 16)
            for c in range(CL):
                last = pe.matmul(bank[7][:], latT[:, c], wlkvT[:, c], start=(c == 0), stop=(c == CL - 1))
            last.then_inc(qkv_in_psum, 1)

            def values(s, r, j):
                if not 0 <= r - 3 < NP:
                    return
                i = s - 3
                first, final = r == 3 and j == 0, r - 3 == NP - 1 and j == 1
                a_hi, a_lo, b_hl = (x_hl[:, (r - 3) % RING, j, part] for part in (A_HI, A_LO, B_HL))
                pe.wait_ge(e_hi_ready, 2 * i + j + 1)
                pe.matmul(U_BANK[0][:], a_hi, e_hi[:, j], start=first, stop=False)
                pe.matmul(U_BANK[0][:], a_lo, e_hi[:, j], start=False, stop=False)
                pe.matmul(U_BANK[1][:], b_hl, e_hi[:, j], start=first, stop=False)
                pe.wait_ge(e_split, 2 * i + j + 1)
                pe.matmul(U_BANK[1][:], b_hl, e_lo[:, j], start=False, stop=final)
                pe.matmul(U_BANK[0][:], a_hi, e_lo[:, j], start=False, stop=final).then_inc(probs_used, 1)

            def scores(dst, hi, lo, split_sem, split):
                for c in range(2):
                    for k, (a, b) in enumerate(((hi, q_hi), (hi, q_lo), (lo, q_hi))):
                        if (c, k) == (0, 2) and split is not None:
                            pe.wait_ge(split_sem, split)
                        last = pe.matmul(dst[:, c * 2 * P:(c + 1) * 2 * P], a[:, c], b[:, c],
                                         start=(k == 0), stop=(k == 2))
                return last

            def step(s, r):
                if 0 <= r - 1 < NP:
                    i = s - 1
                    pe.wait_ge(xT_ready, i + 1)
                    wait_count(pe, k_in_sbuf, i)
                    for j in range(2):
                        products = ((xT[:, j, 0], wk_hi[:, 0]), (xT[:, j, 0], wk_lo[:, 0]), (xT[:, j, 1], wk_hi[:, 1]),
                                    (xT[:, j, 1], wk_lo[:, 1]), (xT_lo[:, j], wk_hi[:, 0]))
                        for n, (a, b) in enumerate(products):
                            if (j, n) == (0, 4):
                                pe.wait_ge(xT_split, i + 1)
                            last = pe.matmul(K_BANK[:, j * DL:(j + 1) * DL], a, b, start=(n == 0), stop=(n == len(products) - 1))
                    last.then_inc(k_in_psum, 1)
                if 0 <= r - 2 < NP:
                    i = s - 2
                    pe.wait_ge(kn_ready, i + 1)
                    wait_count(pe, kT_split, i)
                    for j in range(2):
                        for c in range(2):
                            last = turn(KT_BANK[:, (2 * j + c) * P:(2 * j + c + 1) * P], kn[:, j, c])
                    last.then_inc(kT_in_psum, 1)
                values(s, r, 0)
                if 0 <= r < NP:
                    pe.wait_ge(x_split, s + 1)
                    wait_count(pe, xT_split, s)
                    for j in range(2):
                        turn(XT_BANK[:, 2 * j * P:(2 * j + 1) * P], xh[:, r % 2, j, 0:P])
                        last = turn(XT_BANK[:, (2 * j + 1) * P:(2 * j + 2) * P], x_hl[:, r % RING, j, B_HL].bitcast(F32))
                    last.then_inc(xT_in_psum, 1)
                values(s, r, 1)
                if 0 <= r - 2 < NP:
                    i = s - 2
                    if r == 2:
                        pe.wait_ge(q_split, 1)
                        pe.wait_ge(own_kT_split, 1)
                    pe.wait_ge(kT_hi_ready, i + 1)
                    for j in range(2):
                        wait_count(pe, probs_ready, 2 * i + j - 1)
                        scores(S_BANK[j], kT_hi[:, j], kT_lo[:, j], kT_split, None if j else i + 1).then_inc(scores_ready, 1)

            step(0, 0)
            pe.wait_ge(prep_done, 1)
            step(1, 1)
            pe.wait_ge(qk_normed, 1)
            for a in range(2):
                for c in range(2):
                    last = turn(bank[5 + a][:, c * P:(c + 1) * P], qk[:, a, c * P:(c + 1) * P])
                last.then_inc(qkT_in_psum, 1)
            step(2, 2)
            pe.wait_ge(v_own_ready, 2)
            scores(bank[7], own_hi, own_lo, own_kT_split, 1).then_inc(own_scores, 1)
            run_steps(pe, step, 3, LOOP_FIRST, LOOP_END, LAST)

            keep_up(KEEP_UP[0])
            pe.wait_ge(v_own_ready, 2)
            pe.wait_ge(uT_ready, 2)
            for h in range(H):
                o = bank[7][:, h * (DH + 1):(h + 1) * (DH + 1)]
                pe.matmul(o, e_own[:, h * P:(h + 1) * P], v_own[:, h], start=True, stop=False)
                for c in range(2):
                    last = pe.matmul(o, uT[:, c, h * P:(h + 1) * P], wv[:, c, h], start=False, stop=(c == 1))
            last.then_inc(heads_in_psum, 1)
            keep_up(KEEP_UP[1])
            pe.wait_ge(o_ready, 1)
            for c in range(CL):
                last = turn(bank[2][:, c * P:(c + 1) * P], o_sb[:, c * P:(c + 1) * P])
            last.then_inc(oT_in_psum, 1)
            keep_up(KEEP_UP[2])
            pe.wait_ge(oT_ready, 1)
            pe.wait_ge(w_loaded["woT"], 16)
            pe.wait_ge(small_loaded, 16 * SMALL)
            pe.matmul(bank[4][:, 0:DL], ones_row[:], bo_row[:], start=True, stop=False)
            for c in range(CL):
                last = pe.matmul(bank[4][:, 0:DL], oT[:, c], woT[:, c], start=False, stop=(c == CL - 1))
            last.then_inc(attn_in_psum, 1)

            for l in range(2):
                keep_up(KEEP_UP[3 + l])
                pe.wait_ge(xn_ready, l + 1)
                for c in range(CL):
                    last = turn(bank[2][:, c * P:(c + 1) * P], lat[0][:, c * P:(c + 1) * P])
                last.then_inc(xnT_in_psum, 1)
                pe.wait_ge(xnT_ready, l + 1)
                if l == 0:
                    pe.matmul(bank[3][:, 0:E], ones_row[:], bg_row[:], start=True, stop=False)
                for c in range(CL):
                    last = pe.matmul(bank[3][:, 0:E], latT[:, c], wg[l][:, c], start=(l == 1 and c == 0), stop=(c == CL - 1))
                last.then_inc(logits_in_psum, 1)
                pe.wait_ge(experts_loaded[l], 16 * 8)

                def hidden(e):
                    n = l * E + e
                    wait_count(pe, h_ready, n - 1)
                    for c in range(HC):
                        for d in range(CL):
                            last = pe.matmul(bank[6 + n % 2][:, c * P:(c + 1) * P], w1[l][:, e * CL + d, c * P:(c + 1) * P],
                                             latT[:, d], start=(d == 0), stop=(d == CL - 1))
                    last.then_inc(h_in_psum, 1)

                def expert(e):
                    n = l * E + e
                    wait_count(pe, y_added, n - 1)
                    pe.wait_ge(w2_hi_ready, n + 1)
                    for k, (a, b, split) in enumerate(((h_hi, w2_hi, h_hi_ready), (h_hi, w2_lo, w2_split), (h_lo, w2_hi, h_split))):
                        pe.wait_ge(split, n + 1)
                        for c in range(HC):
                            last = pe.matmul(bank[n % 2][:, 0:DL], a[n % 2][:, c], b[n % 2][:, c],
                                             start=(k == 0 and c == 0), stop=(k == 2 and c == HC - 1))
                    last.then_inc(y_in_psum, 1)

                hidden(0)
                hidden(1)
                expert(0)
                pe.wait_ge(wgt_ready, l + 1)
                turn(bank[4][0:E, 0:P], wgt[:]).then_inc(wgtT_in_psum, 1)
                hidden(2)
                pe.wait_ge(wgtT_ready, l + 1)
                pe.matmul(bank[5][:, 0:DL], wgtT[:], b2[l][:], start=True, stop=True).then_inc(b2_in_psum, 1)
                for e in range(1, E):
                    expert(e)
                    if e + 2 < E:
                        hidden(e + 2)


_OUT = ("out", (1, 128, 256))


def kernel(**inputs):
    import numpy as np
    import concourse.bacc as bacc
    from concourse.bass_utils import run_bass_kernel_spmd

    nc = bacc.Bacc("TRN2", target_bir_lowering=False, num_devices=1)
    layout = {name: np.asarray(value) for name, value in inputs.items()}
    w = {name: layout.pop(f"L0_xattn_{name}") for name in
         ("Wq", "Wkv", "Wlkv", "Wo", "ln_x_g", "ln_x_b", "ln_l_g", "ln_l_b", "qn_g", "kn_g")}
    layout["wqT"], layout["wlkvT"], layout["woT"] = w["Wq"].T, w["Wlkv"].T, w["Wo"].T

    def chunks(a):
        return np.stack([a[:P], np.concatenate([a[P:], a[P:]])])

    layout["wkvT"] = chunks(w["Wkv"].T)
    columns = [w["ln_l_g"].reshape(-1, P).T, w["ln_l_b"].reshape(-1, P).T, chunks(w["ln_x_g"]).T, chunks(w["ln_x_b"]).T,
               np.tile(w["qn_g"], 2)[:, None], np.tile(w["kn_g"], 2)[:, None]]
    for n in ("attn", "ffn"):
        gate = layout.pop(f"L0_{n}_Wg")
        columns.append(gate.reshape(-1, P, gate.shape[1]).transpose(1, 0, 2).reshape(P, -1))
    for n in ("attn", "ffn"):
        columns.append(layout.pop(f"L0_{n}_b1").reshape(-1, P).T)
    layout["columns"] = np.concatenate(columns, axis=1)
    arrays, tensors = {}, {}
    for name, value in layout.items():
        a = np.ascontiguousarray(value)
        arrays[f"in_{name}"] = a
        tensors[name] = nc.dram_tensor(f"in_{name}", a.shape, mybir.dt.from_np(a.dtype), kind="ExternalInput").ap()
    out = nc.dram_tensor(_OUT[0], _OUT[1], F32, kind="ExternalOutput").ap()
    perceiver_block(nc, tensors, out)
    return run_bass_kernel_spmd(nc, [arrays], core_ids=[0]).results[0][_OUT[0]]
```
